# Optimizing a Trainium2 kernel written in Bass

```python
import numpy as np
import jax
import jax.numpy as jnp

def _softmax(x, axis=-1):
    return jax.nn.softmax(x, axis=axis)

def _gelu(x):
    return jax.nn.gelu(x, approximate=True)

def _silu(x):
    return jax.nn.silu(x)

def _sigmoid(x):
    return jax.nn.sigmoid(x)

def _layernorm(x, axis=-1, eps=1e-05):
    m = jnp.mean(x, axis=axis, keepdims=True)
    v = jnp.var(x, axis=axis, keepdims=True)
    return (x - m) / jnp.sqrt(v + eps)

def _scatter_add(tgt, idx, src, axis=0):
    return tgt.at[idx].add(src)

def _segment_sum(src, seg, n):
    return jax.ops.segment_sum(src, seg, n)
kernel_name = 'mk_lm_tower_d1_tok_ids256_r4_664faf'

def setup_inputs(seed: int=0):
    np.random.seed(seed)
    _w = jnp.asarray

    def _rec_inputs():
        import jax
        import jax.numpy as jnp
        _rk = jax.random.key(seed)
        x = jax.random.randint(jax.random.fold_in(_rk, 1), (2, 2048), 0, 64, jnp.int32)
        return x
    x = _rec_inputs()

    def _L0_tok_setup():
        import jax, jax.numpy as jnp
        import numpy as np
        PRIME = 31
        VOCAB = 125000
        NGRAM_SIZES = (2, 3, 4)

        def _ngram_hash(byte_ids, n):
            T = byte_ids.shape[1]
            powers = PRIME ** jnp.arange(n - 1, -1, -1, dtype=jnp.int64) % VOCAB
            windows = jnp.stack([byte_ids[:, i:T - n + 1 + i] for i in range(n)], axis=-1)
            return (windows.astype(jnp.int64) * powers).sum(axis=-1) % VOCAB
        key = jax.random.key(seed)
        k0, k1, k2, k3 = jax.random.split(key, 4)
        byte_ids = jax.random.randint(k0, (8, 1024), 0, 64, dtype=jnp.int64)
        emb_2 = jax.random.normal(k1, (VOCAB, 64), dtype=jnp.float32)
        emb_3 = jax.random.normal(k2, (VOCAB, 64), dtype=jnp.float32)
        emb_4 = jax.random.normal(k3, (VOCAB, 64), dtype=jnp.float32)
        return {'byte_ids': byte_ids, 'emb_2': emb_2, 'emb_3': emb_3, 'emb_4': emb_4}
    _L0_tok_all = _L0_tok_setup()
    _L0_tok_in = {k: v for k, v in _L0_tok_all.items() if k in ('emb_2', 'emb_3', 'emb_4')}
    del _L0_tok_all

    def _L0_attn_setup():
        import jax, jax.numpy as jnp
        import numpy as np
        DIM = 64
        N_SCALES = 4
        PHASES_PER_SCALE = 16
        K_PHASES = N_SCALES * PHASES_PER_SCALE
        B, L = (2, 256)
        key = jax.random.key(seed)
        ks = jax.random.split(key, 16)
        s = 0.02
        d, k = (DIM, K_PHASES)
        return {'x': jax.random.normal(ks[0], (B, L, d), dtype=jnp.float32), 'Wk1': jax.random.normal(ks[1], (d, d), dtype=jnp.float32) * s, 'bk1': jnp.zeros((d,), jnp.float32), 'Wk2': jax.random.normal(ks[2], (d, k), dtype=jnp.float32) * s, 'bk2': jnp.zeros((k,), jnp.float32), 'Wq1': jax.random.normal(ks[3], (d, d), dtype=jnp.float32) * s, 'bq1': jnp.zeros((d,), jnp.float32), 'Wq2': jax.random.normal(ks[4], (d, k), dtype=jnp.float32) * s, 'bq2': jnp.zeros((k,), jnp.float32), 'Wv': jax.random.normal(ks[5], (d, d), dtype=jnp.float32) * s, 'bv': jnp.zeros((d,), jnp.float32), 'ln_w': jnp.ones((d,), jnp.float32), 'ln_b': jnp.zeros((d,), jnp.float32), 'Wo': jax.random.normal(ks[6], (d, d), dtype=jnp.float32) * s, 'bo': jnp.zeros((d,), jnp.float32)}
    _L0_attn_all = _L0_attn_setup()
    _L0_attn_in = {k: v for k, v in _L0_attn_all.items() if k in ('Wk1', 'bk1', 'Wk2', 'bk2', 'Wq1', 'bq1', 'Wq2', 'bq2', 'Wv', 'bv', 'ln_w', 'ln_b', 'Wo', 'bo')}
    del _L0_attn_all

    def _L0_ffn_setup():
        import jax, jax.numpy as jnp
        import numpy as np
        INPUT_WIDTH = 64
        DEPTH = 7
        OUTPUT_WIDTH = 64
        N_NODES = 2 ** (DEPTH + 1) - 1
        key = jax.random.key(seed)
        k_x, k_w1, k_w2 = jax.random.split(key, 3)
        init1 = 1.0 / np.sqrt(INPUT_WIDTH)
        x = jax.random.normal(k_x, (2, 256, INPUT_WIDTH), dtype=jnp.float32)
        w1s = jax.random.uniform(k_w1, (N_NODES, INPUT_WIDTH), jnp.float32, -init1, init1)
        b1s = jnp.zeros((N_NODES,), jnp.float32)
        w2s = jax.random.uniform(k_w2, (N_NODES, INPUT_WIDTH, OUTPUT_WIDTH), jnp.float32, -init1, init1)
        b2s = jnp.zeros((N_NODES, OUTPUT_WIDTH), jnp.float32)
        return {'x': x, 'w1s': w1s, 'b1s': b1s, 'w2s': w2s, 'b2s': b2s}
    _L0_ffn_all = _L0_ffn_setup()
    _L0_ffn_in = {k: v for k, v in _L0_ffn_all.items() if k in ('w1s', 'b1s', 'w2s', 'b2s')}
    del _L0_ffn_all
    return {'x': x, 'L0_tok_emb_2': _L0_tok_in['emb_2'], 'L0_tok_emb_3': _L0_tok_in['emb_3'], 'L0_tok_emb_4': _L0_tok_in['emb_4'], 'L0_attn_Wk1': _L0_attn_in['Wk1'], 'L0_attn_bk1': _L0_attn_in['bk1'], 'L0_attn_Wk2': _L0_attn_in['Wk2'], 'L0_attn_bk2': _L0_attn_in['bk2'], 'L0_attn_Wq1': _L0_attn_in['Wq1'], 'L0_attn_bq1': _L0_attn_in['bq1'], 'L0_attn_Wq2': _L0_attn_in['Wq2'], 'L0_attn_bq2': _L0_attn_in['bq2'], 'L0_attn_Wv': _L0_attn_in['Wv'], 'L0_attn_bv': _L0_attn_in['bv'], 'L0_attn_ln_w': _L0_attn_in['ln_w'], 'L0_attn_ln_b': _L0_attn_in['ln_b'], 'L0_attn_Wo': _L0_attn_in['Wo'], 'L0_attn_bo': _L0_attn_in['bo'], 'L0_ffn_w1s': _L0_ffn_in['w1s'], 'L0_ffn_b1s': _L0_ffn_in['b1s'], 'L0_ffn_w2s': _L0_ffn_in['w2s'], 'L0_ffn_b2s': _L0_ffn_in['b2s']}

def reference(x, L0_tok_emb_2, L0_tok_emb_3, L0_tok_emb_4, L0_attn_Wk1, L0_attn_bk1, L0_attn_Wk2, L0_attn_bk2, L0_attn_Wq1, L0_attn_bq1, L0_attn_Wq2, L0_attn_bq2, L0_attn_Wv, L0_attn_bv, L0_attn_ln_w, L0_attn_ln_b, L0_attn_Wo, L0_attn_bo, L0_ffn_w1s, L0_ffn_b1s, L0_ffn_w2s, L0_ffn_b2s):
    import jax
    import jax.numpy as jnp

    def _L0_tok_ref(byte_ids, emb_2, emb_3, emb_4):
        import jax, jax.numpy as jnp
        import numpy as np
        PRIME = 31
        VOCAB = 125000
        NGRAM_SIZES = (2, 3, 4)

        def _ngram_hash(byte_ids, n):
            T = byte_ids.shape[1]
            powers = PRIME ** jnp.arange(n - 1, -1, -1, dtype=jnp.int64) % VOCAB
            windows = jnp.stack([byte_ids[:, i:T - n + 1 + i] for i in range(n)], axis=-1)
            return (windows.astype(jnp.int64) * powers).sum(axis=-1) % VOCAB
        tables = {2: emb_2, 3: emb_3, 4: emb_4}
        B, T = byte_ids.shape
        D = emb_2.shape[1]
        out = jnp.zeros((B, T, D), dtype=emb_2.dtype)
        for n in NGRAM_SIZES:
            idx = _ngram_hash(byte_ids, n)
            gathered = tables[n][idx]
            out = out + jnp.pad(gathered, ((0, 0), (n - 1, 0), (0, 0)))
        return out / (len(NGRAM_SIZES) + 1)

    def _L0_attn_ref(x, Wk1, bk1, Wk2, bk2, Wq1, bq1, Wq2, bq2, Wv, bv, ln_w, ln_b, Wo, bo):
        import jax, jax.numpy as jnp
        import numpy as np
        DIM = 64
        N_SCALES = 4
        PHASES_PER_SCALE = 16
        K_PHASES = N_SCALES * PHASES_PER_SCALE
        B, L = (2, 256)
        Bb, Ll, D = x.shape
        K = K_PHASES
        freq = jnp.repeat(2.0 ** jnp.arange(N_SCALES, dtype=jnp.float32), PHASES_PER_SCALE)

        def encode(W1, b1, W2, b2):
            h = jax.nn.gelu(x @ W1 + b1, approximate=False)
            return jnp.tanh(h @ W2 + b2)
        key_phase = encode(Wk1, bk1, Wk2, bk2) * freq * jnp.pi
        query_phase = encode(Wq1, bq1, Wq2, bq2) * freq * jnp.pi
        key_phasor = jnp.cos(key_phase) + 1j * jnp.sin(key_phase)
        query_conj = jnp.cos(query_phase) - 1j * jnp.sin(query_phase)
        V = (x @ Wv + bv).astype(jnp.complex64)
        bound = key_phasor[..., None] * V[:, :, None, :]
        memory = jnp.cumsum(bound, axis=1)
        retrieved = jnp.real(jnp.sum(memory * query_conj[..., None], axis=2))
        positions = jnp.arange(1, Ll + 1, dtype=jnp.float32)
        retrieved = retrieved / jnp.sqrt(positions * K)[None, :, None]
        mu = jnp.mean(retrieved, axis=-1, keepdims=True)
        var = jnp.var(retrieved, axis=-1, keepdims=True)
        normed = (retrieved - mu) / jnp.sqrt(var + 1e-05) * ln_w + ln_b
        return x + normed @ Wo + bo

    def _L0_ffn_ref(x, w1s, b1s, w2s, b2s):
        import jax, jax.numpy as jnp
        import numpy as np
        INPUT_WIDTH = 64
        DEPTH = 7
        OUTPUT_WIDTH = 64
        N_NODES = 2 ** (DEPTH + 1) - 1
        B, S, D = x.shape
        flat_x = x.reshape(B * S, D)
        T = flat_x.shape[0]
        current = jnp.zeros((T,), dtype=jnp.int32)
        all_nodes = []
        all_logits = []
        for _ in range(DEPTH + 1):
            all_nodes.append(current)
            score = jnp.einsum('td,td->t', flat_x, w1s[current]) + b1s[current]
            all_logits.append(score)
            choice = ((jnp.sign(score) + 1.0) / 2.0).astype(jnp.int32)
            current = current * 2 + choice + 1
        logits = jnp.stack(all_logits, axis=1)
        path_weights = jax.nn.gelu(jnp.abs(logits), approximate=False)
        out = jnp.zeros((T, OUTPUT_WIDTH), dtype=x.dtype)
        for i in range(DEPTH + 1):
            nodes_i = all_nodes[i]
            t_i = jnp.einsum('td,tdo->to', flat_x, w2s[nodes_i]) + b2s[nodes_i]
            out = out + t_i * path_weights[:, i][:, None]
        return out.reshape(B, S, OUTPUT_WIDTH)
    h = _L0_tok_ref(x, L0_tok_emb_2, L0_tok_emb_3, L0_tok_emb_4)
    h = h + _L0_attn_ref(_layernorm(h, axis=-1), L0_attn_Wk1, L0_attn_bk1, L0_attn_Wk2, L0_attn_bk2, L0_attn_Wq1, L0_attn_bq1, L0_attn_Wq2, L0_attn_bq2, L0_attn_Wv, L0_attn_bv, L0_attn_ln_w, L0_attn_ln_b, L0_attn_Wo, L0_attn_bo)
    h = h + _L0_ffn_ref(_layernorm(h, axis=-1), L0_ffn_w1s, L0_ffn_b1s, L0_ffn_w2s, L0_ffn_b2s)
    return h

_drawn_inputs = setup_inputs


def setup_inputs(seed=0):
    import zlib

    import numpy as np

    out = dict(_drawn_inputs(seed))
    spreads = {'L0_attn_bk1': (0.0, 0.564),
     'L0_attn_bk2': (0.0, 0.36),
     'L0_attn_bq1': (0.0, 0.764),
     'L0_attn_bq2': (0.0, 0.361),
     'L0_attn_bv': (0.0, 0.1),
     'L0_attn_ln_w': (1.0, 0.2),
     'L0_attn_ln_b': (0.0, 0.1),
     'L0_attn_bo': (0.0, 0.1),
     'L0_ffn_b1s': (0.0, 0.1),
     'L0_ffn_b2s': (0.0, 0.1)}
    factors = {'L0_attn_Wk1': 3.116, 'L0_attn_Wk2': 3.714, 'L0_attn_Wq1': 8.0, 'L0_attn_Wq2': 5.641}
    for name, (base, spread) in spreads.items():
        noise = np.random.default_rng([zlib.crc32(name.encode()), seed]).standard_normal(out[name].shape)
        drawn = base * np.exp(spread * noise) if base else spread * noise
        out[name] = jnp.asarray(drawn.astype(out[name].dtype))
    for name, factor in factors.items():
        out[name] = (out[name] * factor).astype(out[name].dtype)
    return out
```

```python
from contextlib import ExitStack

import concourse.bass as bass
from concourse import mybir

F32 = mybir.dt.float32
BF16 = mybir.dt.bfloat16
I32 = mybir.dt.int32
ALU = mybir.AluOpType
ACT = mybir.ActivationFunctionType
AXX = mybir.AxisListType.X

P = 128
B, T, D = 2, 2048, 64
K = 64
VOCAB = 125000
PRIME = 31
EPS = 1e-5
NT = B * T // P
TB = T // P
GT = 4
NG = NT // GT
GN = GT * P
NODES = 255
LEVELS = 8
PAR = 64
PW = D + 9
OVP = 32
SLOTS = (PAR + OVP) * P
OV0 = PAR * P
FAR = 1 << 16
TWO_PI = 6.283185
ROUND = 12582912.0
W01, W23, W45, W7, W6 = 0, 2, 10, 42, 106
NBLK = 170

C_ID, C_MASK, C_IOTA, C_FREQ, C_OFF, C_EPS = 0, 128, 256, 384, 385, 386
C_W1, C_W2, C_WV, C_WO, C_TREE, C_B1, C_B2K, C_B2Q, C_LNW, C_LNB = 402, 530, 658, 722, 786, 1041, 1042, 1043, 1044, 1045
C_ALL = 1046


class Chain:

    def __init__(self, eng, sem):
        self.eng, self.sem, self.n = eng, sem, 0

    def put(self, ins):
        self.n += 1
        ins.then_inc(self.sem, 1)

    def settle(self):
        self.eng.wait_ge(self.sem, self.n)


def build(nc, x, emb2, emb3, emb4, small, nodes, out):
    with ExitStack() as ctx:
        def sb(name, shape, dt=F32):
            return ctx.enter_context(nc.sbuf_tensor(name, shape, dt))

        def psum(name, shape):
            return ctx.enter_context(nc.psum_tensor(name, shape, F32))

        def sem(name):
            return ctx.enter_context(nc.semaphore(name))

        tp = psum("tp", [P, 512])
        mm = psum("mm", [P, 2, 512])
        vr = psum("vr", [P, 2, GT, D])
        sc = psum("sc", [P, GT, P])
        ws = psum("ws", [P, 2, GT, D])
        tree = psum("tree", [P, GT, 256])

        cw = sb("cw", [P, C_ALL])
        ident, mask = cw[:, C_ID:C_ID + P], cw[:, C_MASK:C_MASK + P]
        iota = cw[:, C_IOTA:C_IOTA + P]
        tri = sb("tri", [P, P], BF16)
        onesb = sb("onesb", [P, P], BF16)
        lw = sb("lw", [D + 1, D + 1])
        wo_s = sb("wo_s", [D + 1, D])
        xi = sb("xi", [NT, 3 + P], I32)
        xf = sb("xf", [NT, 3 + P])
        hs = sb("hs", [NT, 3, P])
        hq = sb("hq", [NT, 3, P])
        idx = sb("idx", [P, 3, NT], I32)
        emb = sb("emb", [P, NT, 3, D])
        tsum = sb("tsum", [P, 2, GT, D])
        bn = sb("bn", [P, GT, 6])
        mv = sb("mv", [P, GT, 2])
        rv = sb("rv", [P, GT])
        ri = sb("ri", [P, GT], I32)
        ry = sb("ry", [P, GT])
        ra = sb("ra", [P, GT])
        rb = sb("rb", [P, GT])
        xln = sb("xln", [P, 2, GT, D])
        h2 = sb("h2", [P, NT, D])
        xT = sb("xT", [D + 1, 2, GN])
        hid = sb("hid", [P, GN])
        ph = sb("ph", [P, 2, GN])
        pr = sb("pr", [P, 2, GN])
        pu = sb("pu", [P, 2, GN])
        feat = sb("feat", [P, 2, 2, GN])
        kft = sb("kft", [P, GT, P])
        vs = sb("vs", [P, 2, GT, D])
        pt = sb("pt", [P, GT, P])
        st = sb("st", [P, 2 * GT, D])
        nrm = sb("nrm", [P, GT, D])
        nT = sb("nT", [D + 1, GN])
        fT = sb("fT", [D + 1, GN])
        pay = sb("pay", [P, NT, PW])
        lg = sb("lg", [P, GT, 9])
        la = sb("la", [P, 2, GT, 9])
        cur = sb("cur", [P, GT])
        cur2 = sb("cur2", [P, GT])
        rgt = sb("rgt", [P, GT])
        msk = sb("msk", [P, GT, 64])
        mks = sb("mks", [P, GT, P])
        one = sb("one", [P, NT, PAR], BF16)
        lsum = sb("lsum", [P, PAR], BF16)
        lpart = sb("lpart", [P, PAR], BF16)
        rtmp = sb("rtmp", [P, GT, PAR])
        rank = sb("rank", [P, NT])
        row0 = sb("row0", [P, NT])
        far = sb("far", [P, GT])
        idx1 = sb("idx1", [P, NT], I32)
        wf = sb("wf", [P, NBLK, D])
        xs = emb[:].rearrange("p t j d -> p (t j d)")[:, 0:PAR * PW].rearrange("p (a w) -> p a w", w=PW)
        xov = sb("xov", [P, OVP, PW])
        z = sb("z", [P, 2, 640])
        zT = sb("zT", [P, 2, 640])
        ys = sb("ys", [P, PAR, D])
        yov = sb("yov", [P, OVP, D])
        ovr = sb("ovr", [P, PAR])
        ovi = sb("ovi", [P, PAR], I32)
        ovinc = sb("ovinc", [P, PAR])
        ovexc = sb("ovexc", [P, PAR])
        onesf = sb("onesf", [P, PAR])
        occ = sb("occ", [PAR, 1])
        oci = sb("oci", [PAR, 1], I32)
        oce = sb("oce", [PAR, 1])
        cmp = sb("cmp", [PAR, OVP])
        pgi = sb("pgi", [1, OVP + 1], I32)
        tk = sb("tk", [P, 6, NT])
        tki = sb("tki", [P, NT], I32)
        idx2 = sb("idx2", [P, NT], I32)
        idx3 = sb("idx3", [P, NT], I32)
        yg = sb("yg", [P, NT, D])

        slots = nc.dram_tensor("slots", (SLOTS, PW), F32, kind="Internal").ap()
        ydram = nc.dram_tensor("ydram", (SLOTS, D), F32, kind="Internal").ap()

        s_small = sem("s_small")
        s_ids = sem("s_ids")
        s_wf = sem("s_wf")
        s_clear = sem("s_clear")
        s_slot0 = sem("s_slot0")
        s_halo = sem("s_halo")
        dv = sem("dv")
        d_hash, p_hash, d_idx = sem("d_hash"), sem("p_hash"), sem("d_idx")
        d_lw, p_lw, d_wo = sem("d_lw"), sem("p_lw"), sem("d_wo")
        g_emb = [sem(f"g_emb{g}") for g in range(NG)]
        g_scat = [sem(f"g_scat{g}") for g in range(NG)]
        d_xln, d_phase, d_mask, d_state, d_nrm, d_xf, d_walk, d_rank, d_one, d_slot = (
            sem(n) for n in ("d_xln", "d_phase", "d_mask", "d_state", "d_nrm", "d_xf", "d_walk", "d_rank", "d_one", "d_slot"))
        p_xT, p_hid, p_v, p_sc, p_phk, p_phq, p_retr, p_st, p_nT, p_wo, p_kft, p_fT, p_tree, p_rank = (
            sem(n) for n in ("p_xT", "p_hid", "p_v", "p_sc", "p_phk", "p_phq", "p_retr", "p_st", "p_nT", "p_wo", "p_kft", "p_fT", "p_tree", "p_rank"))
        a_xT, a_hid, a_v, a_tk, a_tq, a_w, a_nT, a_sin, a_kft, a_fT = (
            sem(n) for n in ("a_xT", "a_hid", "a_v", "a_tk", "a_tq", "a_w", "a_nT", "a_sin", "a_kft", "a_fT"))
        p_cnt, d_ovc, p_ovi, d_cmp, p_pg, d_pg, d_idx2 = (
            sem(n) for n in ("p_cnt", "d_ovc", "p_ovi", "d_cmp", "p_pg", "d_pg", "d_idx2"))
        g_second = sem("g_second")
        s_xs, s_xov = sem("s_xs"), sem("s_xov")
        d_z, p_tr, a_zT, p_mm, d_y = (sem(n) for n in ("d_z", "p_tr", "a_zT", "p_mm", "d_y"))
        s_y, s_yov, s_stored = sem("s_y"), sem("s_yov"), sem("s_stored")
        g_y = [sem(f"g_y{g}") for g in range(NG)]
        d_out, s_out = sem("d_out"), sem("s_out")

        def bc(ap, shape):
            return ap.unsqueeze(2).to_broadcast(shape)

        def bc_mid(ap, shape):
            return ap.unsqueeze(1).to_broadcast(shape)

        def tile(t, n=P):
            return slice(t * P, t * P + n)

        CH = 8
        ids = x.rearrange("b t -> (b t)")
        wcol = {"p01": W01, "p23": W23, "p45": W45, "p7": W7, "p6": W6}

        block = ctx.enter_context(nc.Block())

        @block.sync
        def _(sp):
            rows = ids.rearrange("(n p) -> n p", p=P)
            sp.dma_start(xi[0:NT, 3:3 + P], rows).then_inc(s_ids, 16)
            sp.dma_start(xi[1:NT, 0:3], rows[0:NT - 1, P - 3:P]).then_inc(s_ids, 16)
            sp.dma_start(cw[:], small).then_inc(s_small, 16)
            sp.wait_ge(s_clear, 1)
            flat = slots.rearrange("(q a) d -> q (a d)", q=P)
            width, zero = SLOTS // P * PW, yov[:].rearrange("p a d -> p (a d)")
            n0 = 0
            for c0 in range(0, width, OVP * D):
                n = min(OVP * D, width - c0)
                sp.dma_start(flat[:, c0:c0 + n], zero[:, 0:n]).then_inc(s_slot0, 16)
                n0 += 1
            assert n0 == 4
            sp.dma_start(ydram[OV0:SLOTS].rearrange("(q a) d -> q a d", q=P), yov[:]).then_inc(s_slot0, 16)
            sp.dma_start(wf[:].rearrange("p b d -> p (b d)"), nodes).then_inc(s_wf, 16)
            for g in range(NG):
                sp.wait_ge(g_scat[g], 16 * GT)
            page = slots[0:OV0].rearrange("(q a) d -> q a d", q=P)
            for c in range(PAR // CH):
                if c:
                    sp.wait_ge(s_xs, 16 * c)
                sp.dma_start(xs[:, c * CH:(c + 1) * CH, :], page[:, c * CH:(c + 1) * CH, :]).then_inc(s_xs, 16)
            sp.wait_ge(g_second, 16 * NT)
            sp.dma_start(xov[:], slots[OV0:SLOTS].rearrange("(q a) d -> q a d", q=P)).then_inc(s_xov, 16)
            ypage = ydram[0:OV0].rearrange("(q a) d -> q a d", q=P)
            for c in range(PAR // CH):
                sp.wait_ge(d_y, (c + 1) * CH)
                sp.dma_start(ypage[:, c * CH:(c + 1) * CH, :], ys[:, c * CH:(c + 1) * CH, :]).then_inc(s_y, 16)
            yo = ydram[OV0:SLOTS].rearrange("(q a) d -> q a d", q=P)
            npg = sp.value_load(pgi[0:1, OVP:OVP + 1], min_val=1, max_val=OVP)
            with sp.Fori(0, npg) as j:
                sp.wait_ge(d_y, j + (PAR + 1))
                sp.dma_start(yo[:, bass.ds(j, 1), :], yov[:, bass.ds(j, 1), :]).then_inc(s_yov, 16)
            sp.wait_ge(s_y, 16 * (PAR // CH))
            sp.wait_ge(s_yov, npg * 16)
            sp.sem_inc(s_stored, 1)
            for g in range(NG):
                sp.wait_ge(d_out, g + 1)
                b, t0 = divmod(g * GT, TB)
                sp.dma_start(out[b].rearrange("(t p) d -> p t d", p=P)[:, t0:t0 + GT, :],
                             yg[:, g * GT:(g + 1) * GT, :]).then_inc(s_out, 16)
            sp.wait_ge(s_out, 16 * NG)

        @block.gpsimd
        def _(pool):
            pool.memset(yov[:], 0.0).then_inc(s_clear, 1)
            pool.memset(z[:], 0.0).then_inc(s_clear, 1)

            def gather(g):
                for t in range(g * GT, (g + 1) * GT):
                    for j, table in enumerate((emb2, emb3, emb4)):
                        pool.indirect_dma_start(emb[:, t, j, :], None, table,
                                                bass.IndirectOffsetOnAxis(idx[:, j, t:t + 1], 0)).then_inc(g_emb[g], 16)

            def scatter(g):
                pool.wait_ge(d_slot, g + 1)
                pool.wait_ge(a_w, g + 1)
                for t in range(g * GT, (g + 1) * GT):
                    pool.indirect_dma_start(slots, bass.IndirectOffsetOnAxis(idx1[:, t:t + 1], 0), pay[:, t, :], None,
                                            bounds_check=SLOTS - 1, oob_is_err=False).then_inc(g_scat[g], 16)

            pool.wait_ge(d_idx, 1)
            for g in range(NG + 3):
                if g < NG:
                    gather(g)
                if g == 3:
                    pool.wait_ge(s_slot0, 80)
                if g >= 3:
                    scatter(g - 3)
            pool.wait_ge(d_idx2, 1)
            for t in range(NT):
                pool.indirect_dma_start(slots, bass.IndirectOffsetOnAxis(idx2[:, t:t + 1], 0), pay[:, t, :], None,
                                        bounds_check=SLOTS - 1, oob_is_err=False).then_inc(g_second, 16)
            pool.wait_ge(s_stored, 1)
            for t in range(NT):
                pool.indirect_dma_start(yg[:, t, :], None, ydram,
                                        bass.IndirectOffsetOnAxis(idx3[:, t:t + 1], 0)).then_inc(g_y[t // GT], 16)

        @block.scalar
        def _(act):
            act.wait_ge(s_small, 16)

            def front(g):
                par = g % 2
                act.wait_ge(p_xT, g + 1)
                if g == 0:
                    act.wait_ge(dv, 4)
                act.copy(xT[0:D, par, :], tp[0:D, :]).then_inc(a_xT, 1)
                act.wait_ge(p_hid, g + 1)
                act.activation(hid[:], mm[:, 0, :], ACT.Gelu, bias=cw[:, C_B1:C_B1 + 1]).then_inc(a_hid, 1)
                act.wait_ge(p_v, g + 1)
                act.copy(vs[:, par], vr[:, 0]).then_inc(a_v, 1)
                act.wait_ge(p_phk, g + 1)
                act.activation(ph[:, 0, :], mm[:, 1, :], ACT.Tanh, bias=cw[:, C_B2K:C_B2K + 1]).then_inc(a_tk, 1)
                act.wait_ge(p_phq, g + 1)
                act.activation(ph[:, 1, :], mm[:, 0, :], ACT.Tanh, bias=cw[:, C_B2Q:C_B2Q + 1]).then_inc(a_tq, 1)

            def weights(g):
                act.wait_ge(d_walk, g + 1)
                act.activation(pay[:, g * GT:(g + 1) * GT, D:PW], la[:, g % 2], ACT.Gelu).then_inc(a_w, 1)

            def turn_nrm(g):
                act.wait_ge(p_nT, g + 1)
                act.copy(nT[0:D, :], tp[0:D, :]).then_inc(a_nT, 1)

            def features(g):
                act.wait_ge(d_phase, g + 1)
                act.activation(feat[:, g % 2], pr[:], ACT.Sin, scale=TWO_PI).then_inc(a_sin, 1)
                act.wait_ge(p_kft, g + 1)
                act.copy(kft[:], mm[:, 1, :].rearrange("p (t f) -> p t f", t=GT)).then_inc(a_kft, 1)

            def turn_xf(g):
                act.wait_ge(p_fT, g + 1)
                act.copy(fT[0:D, :], tp[0:D, :]).then_inc(a_fT, 1)

            for k in range(NG + 2):
                if k < NG:
                    front(k)
                if k >= 2:
                    weights(k - 2)
                if 1 <= k <= NG:
                    turn_nrm(k - 1)
                if k < NG:
                    features(k)
                if 1 <= k <= NG:
                    turn_xf(k - 1)

            def z_out(n, b, first):
                act.wait_ge(p_tr, n + 1)
                if not first:
                    act.wait_ge(p_mm, n - 1)
                src = tree[:].rearrange("p a b -> p (a b)") if b == 0 else mm[:].rearrange("p a b -> p (a b)")
                act.copy(zT[:, b, :], src[:, 0:640]).then_inc(a_zT, 1)

            act.preload_act_table_set("gelu_and_others")
            z_out(0, 0, True)
            z_out(1, 1, True)
            with act.Fori(1, PAR // 2) as i:
                z_out(i * 2, 0, False)
                z_out(i * 2 + 1, 1, False)
            npg = act.value_load(pgi[0:1, OVP:OVP + 1], min_val=1, max_val=OVP)
            with act.Fori(0, npg) as j:
                act.wait_ge(p_tr, j + (PAR + 1))
                act.wait_ge(p_mm, j + PAR)
                act.copy(zT[:, 0, :], tree[:].rearrange("p a b -> p (a b)")[:, 0:640]).then_inc(a_zT, 1)

        @block.tensor
        def _(pe):
            pe.wait_ge(s_small, 16)
            w1 = cw[0:D, C_W1:C_W1 + P]
            w2k, w2q = cw[0:D, C_W2:C_W2 + P], cw[D:P, C_W2:C_W2 + P]
            wv = cw[0:D + 1, C_WV:C_WV + D]
            wtree = cw[0:D + 1, C_TREE:C_TREE + NODES]

            pe.wait_ge(d_hash, 1)
            for j in range(3):
                last = pe.transpose(tp[:, j * NT:(j + 1) * NT], hs[:, j, :], ident[0:NT, 0:NT])
            last.then_inc(p_hash, 1)
            pe.wait_ge(d_lw, 1)
            pe.matmul(ws[0:D + 1, 0, 0, :], lw[:], cw[0:D + 1, C_WO:C_WO + D], start=True, stop=True).then_inc(p_lw, 1)

            def turn_x(g):
                pe.wait_ge(d_xln, g + 1)
                if g == 0:
                    pe.wait_ge(d_idx, 1)
                else:
                    pe.wait_ge(a_fT, g - 1) if g > 1 else None
                for t in range(GT):
                    last = pe.transpose(tp[0:D, tile(t)], xln[:, g % 2, t, :], ident)
                last.then_inc(p_xT, 1)

            def hidden(g):
                pe.wait_ge(a_xT, g + 1)
                if g:
                    pe.wait_ge(a_tq, g)
                pe.matmul(mm[:, 0, :], w1, xT[0:D, g % 2, :], start=True, stop=True).then_inc(p_hid, 1)
                if g > 1:
                    pe.wait_ge(d_nrm, g - 1)
                for t in range(GT):
                    last = pe.matmul(vr[:, 0, t, :], xT[:, g % 2, tile(t)], wv, start=True, stop=True)
                last.then_inc(p_v, 1)

            def scores(g):
                pe.wait_ge(a_sin, g + 1)
                if g:
                    pe.wait_ge(d_mask, g)
                for t in range(GT):
                    last = pe.matmul(sc[:, t, :], feat[:, g % 2, 0, tile(t)], feat[:, g % 2, 1, tile(t)], start=True, stop=True)
                last.then_inc(p_sc, 1)

            def phases(g):
                pe.wait_ge(a_hid, g + 1)
                if g:
                    pe.wait_ge(a_kft, g)
                pe.matmul(mm[:, 1, :], w2k, hid[0:D, :], start=True, stop=True).then_inc(p_phk, 1)
                pe.matmul(mm[:, 0, :], w2q, hid[D:P, :], start=True, stop=True).then_inc(p_phq, 1)

            def attend(g):
                pe.wait_ge(a_kft, g + 1)
                pe.wait_ge(a_v, g + 1)
                pe.wait_ge(d_wo, 1) if g == 0 else pe.wait_ge(d_xf, g)
                for t in range(GT):
                    last = pe.matmul(ws[:, 1, t, :], kft[:, t, :], vs[:, g % 2, t, :], start=True, stop=True)
                last.then_inc(p_st, 1)
                pe.wait_ge(d_mask, g + 1)
                pe.wait_ge(a_v, min(g + 2, NG))
                for t in range(GT):
                    n = g * GT + t
                    first = n % TB == 0
                    last = pe.matmul(vr[:, 1, t, :], pt[:, t, :], vs[:, g % 2, t, :], start=True, stop=first)
                    if not first:
                        pe.wait_ge(d_state, n)
                        last = pe.matmul(vr[:, 1, t, :], feat[:, g % 2, 1, tile(t)], st[:, n % (2 * GT), :],
                                         start=False, stop=True)
                last.then_inc(p_retr, 1)

            def turn_nrm(g):
                pe.wait_ge(d_nrm, g + 1)
                pe.wait_ge(a_xT, min(g + 2, NG))
                for t in range(GT):
                    last = pe.transpose(tp[0:D, tile(t)], nrm[:, t, :], ident)
                last.then_inc(p_nT, 1)

            def project(g):
                pe.wait_ge(a_nT, g + 1)
                pe.wait_ge(d_state, min(GT * (g + 1), NT - 1))
                for t in range(GT):
                    last = pe.matmul(ws[:, 0, t, :], nT[:, tile(t)], wo_s[:], start=True, stop=True)
                last.then_inc(p_wo, 1)

            def turn_keys(g):
                pe.wait_ge(a_sin, g + 1)
                pe.wait_ge(a_tk, g + 1)
                for t in range(GT):
                    last = pe.transpose(mm[:, 1, tile(t)], feat[:, g % 2, 0, tile(t)], ident)
                last.then_inc(p_kft, 1)

            def node_scores(g):
                pe.wait_ge(d_xf, g + 1)
                pe.wait_ge(a_nT, g + 1)
                for t in range(GT):
                    last = pe.transpose(tp[0:D, tile(t)], pay[:, g * GT + t, 0:D], ident)
                last.then_inc(p_fT, 1)
                pe.wait_ge(a_fT, g + 1)
                if g:
                    pe.wait_ge(d_rank, g)
                for t in range(GT):
                    last = pe.matmul(tree[:, t, 0:NODES], fT[:, tile(t)], wtree, start=True, stop=True)
                last.then_inc(p_tree, 1)

            def ranks(g):
                pe.wait_ge(d_one, g + 1)
                for t in range(GT):
                    parts = [(tri[:], one[:, g * GT + t, :])] + [(onesb[:], one[:, g * GT + u, :]) for u in range(t)]
                    if g:
                        parts.append((onesb[:], lsum[:]))
                    for n, (a, b) in enumerate(parts):
                        last = pe.matmul(tree[:, 0, t * PAR:(t + 1) * PAR] , a, b, start=(n == 0), stop=(n == len(parts) - 1))
                last.then_inc(p_rank, 1)

            for k in range(NG + 2):
                if k < NG:
                    turn_x(k)
                    hidden(k)
                if 1 <= k <= NG:
                    scores(k - 1)
                if k < NG:
                    phases(k)
                if 1 <= k <= NG:
                    attend(k - 1)
                if k >= 2:
                    ranks(k - 2)
                if 1 <= k <= NG:
                    turn_nrm(k - 1)
                    project(k - 1)
                if k < NG:
                    turn_keys(k)
                if 1 <= k <= NG:
                    node_scores(k - 1)

            pe.wait_ge(d_rank, NG)
            pe.matmul(vr[:, 0, 0, :], onesb[:], lsum[:], start=True, stop=True)
            pe.matmul(vr[0:PAR, 0, 1, 0:1], lsum[:], onesb[:, 0:1], start=True, stop=True).then_inc(p_cnt, 1)
            pe.wait_ge(d_ovc, 1)
            pe.matmul(vr[0:PAR, 0, 1, 1:2], cw[0:PAR, C_MASK:C_MASK + PAR], oce[:], start=True, stop=True).then_inc(p_ovi, 1)
            pe.wait_ge(d_cmp, 1)
            pe.matmul(vr[0:1, 0, 2, 0:OVP], onesf[0:PAR, 0:1], cmp[:], start=True, stop=True).then_inc(p_pg, 1)

            zps = [tree[:].rearrange("p a b -> p (a b)"), mm[:].rearrange("p a b -> p (a b)")]
            yps = [vr[:, 1, 0, :], ws[:, 0, 0, :]]

            def turn_z(n, b, first=False):
                pe.wait_ge(d_z, n + 1)
                if not first:
                    pe.wait_ge(a_zT, n - 1)
                for c in range(5):
                    last = pe.transpose(zps[b][:, tile(c)], z[:, b, tile(c)], ident)
                last.then_inc(p_tr, 1)

            def node_products(n, b, blocks, first=False):
                pe.wait_ge(a_zT, n + 1)
                if not first:
                    pe.wait_ge(d_y, n - 1)
                for c, blk in enumerate(blocks):
                    rows = P if c < 4 else PW
                    last = pe.matmul(yps[b], zT[0:rows, b, tile(c)],
                                     wf[0:rows, blk, :] if isinstance(blk, int) else
                                     wf[0:rows, bass.ds(blk, 1), :].rearrange("p a d -> p (a d)"),
                                     start=(c == 0), stop=(c == 4))
                last.then_inc(p_mm, 1)

            def blocks(i, b):
                return [(i >> 4) + W01, (i >> 2) + W23, i + W45, i * 2 + (W7 + b), i * 2 + (W6 + b)]

            pe.wait_ge(s_wf, 16)
            turn_z(0, 0, True)
            turn_z(1, 1, True)
            node_products(0, 0, blocks(0, 0), True)
            with pe.Fori(1, PAR // 2) as i:
                turn_z(i * 2, 0)
                node_products(i * 2 - 1, 1, blocks(i - 1, 1))
                turn_z(i * 2 + 1, 1)
                node_products(i * 2, 0, blocks(i, 0))
            node_products(PAR - 1, 1, blocks(PAR // 2 - 1, 1))
            pe.wait_ge(d_pg, 1)
            npg = pe.value_load(pgi[0:1, OVP:OVP + 1], min_val=1, max_val=OVP)
            with pe.Fori(0, npg) as j:
                par = pe.value_load(pgi[0:1, bass.ds(j, 1)], min_val=0, max_val=PAR - 1)
                pe.wait_ge(d_z, j + (PAR + 1))
                pe.wait_ge(a_zT, j + PAR)
                for c in range(5):
                    last = pe.transpose(zps[0][:, tile(c)], z[:, 0, tile(c)], ident)
                last.then_inc(p_tr, 1)
                pe.wait_ge(a_zT, j + (PAR + 1))
                pe.wait_ge(d_y, j + PAR)
                for c, blk in enumerate([(par >> 5) + W01, (par >> 3) + W23, (par >> 1) + W45, par + W7, par + W6]):
                    rows = P if c < 4 else PW
                    last = pe.matmul(yps[0], zT[0:rows, 0, tile(c)],
                                     wf[0:rows, bass.ds(blk, 1), :].rearrange("p a d -> p (a d)"),
                                     start=(c == 0), stop=(c == 4))
                last.then_inc(p_mm, 1)

        @block.vector
        def _(dve):
            ch = Chain(dve, dv)
            put, settle = ch.put, ch.settle

            put(dve.memset(xT[D:D + 1, :, :], 1.0))
            put(dve.memset(nT[D:D + 1, :], 1.0))
            put(dve.memset(fT[D:D + 1, :], 1.0))
            put(dve.memset(xi[0:1, 0:3], 0))
            put(dve.memset(onesb[:], 1.0))
            put(dve.memset(onesf[:], 1.0))
            put(dve.memset(lsum[:], 0.0))
            settle()

            dve.wait_ge(s_ids, 32)
            put(dve.tensor_copy(xf[:], xi[:]))
            settle()
            h = hs
            put(dve.scalar_tensor_tensor(out=h[:, 0, :], in0=xf[:, 2:2 + P], scalar=float(PRIME), in1=xf[:, 3:3 + P],
                                         op0=ALU.mult, op1=ALU.add))
            settle()
            put(dve.scalar_tensor_tensor(out=h[:, 1, :], in0=xf[:, 1:1 + P], scalar=float(PRIME ** 2), in1=h[:, 0, :],
                                         op0=ALU.mult, op1=ALU.add))
            settle()
            put(dve.scalar_tensor_tensor(out=h[:, 2, :], in0=xf[:, 0:P], scalar=float(PRIME ** 3), in1=h[:, 1, :],
                                         op0=ALU.mult, op1=ALU.add))
            settle()
            put(dve.tensor_scalar(hq[:], h[:], 1.0 / VOCAB, ROUND, ALU.mult, ALU.add))
            settle()
            put(dve.tensor_scalar(hq[:], hq[:], ROUND, float(VOCAB), ALU.subtract, ALU.mult))
            settle()
            put(dve.tensor_tensor(h[:], h[:], hq[:], ALU.subtract))
            settle()
            put(dve.tensor_scalar(hq[:], h[:], 0.0, float(VOCAB), ALU.is_lt, ALU.mult))
            settle()
            dve.tensor_tensor(h[:], h[:], hq[:], ALU.add).then_inc(d_hash, 1)

            dve.wait_ge(s_small, 16)
            put(dve.tensor_tensor(tri[:], mask, ident, ALU.subtract))
            put(dve.tensor_scalar(lw[:], cw[0:D + 1, C_ID:C_ID + D + 1], cw[0:D + 1, C_LNW:C_LNW + 1], None, ALU.mult))
            settle()
            dve.tensor_copy(lw[:, D:D + 1], cw[0:D + 1, C_LNB:C_LNB + 1]).then_inc(d_lw, 1)
            dve.wait_ge(p_hash, 1)
            dve.tensor_copy(idx[:], tp[:, 0:3 * NT].rearrange("p (j t) -> p j t", j=3)).then_inc(d_idx, 1)
            dve.wait_ge(p_lw, 1)
            dve.tensor_copy(wo_s[:], ws[0:D + 1, 0, 0, :]).then_inc(d_wo, 1)

            def layernorm(src, dst, eps, done):
                for t in range(GT):
                    put(dve.bn_stats(bn[:, t, :], src[:, t, :]))
                settle()
                for t in range(GT):
                    put(dve.bn_aggr(mv[:, t, :], bn[:, t, :]))
                settle()
                if isinstance(eps, float):
                    put(dve.tensor_scalar(rv[:], mv[:, :, 1], eps, None, ALU.add))
                else:
                    put(dve.tensor_tensor(rv[:], mv[:, :, 1], eps, ALU.add))
                settle()
                put(dve.tensor_single_scalar(ri[:], rv[:].bitcast(I32), 1, op=ALU.logical_shift_right))
                settle()
                put(dve.tensor_scalar(ry[:].bitcast(I32), ri[:], -1.0, float(0x5F3759DF), ALU.mult, ALU.add))
                settle()
                for _ in range(3):
                    put(dve.tensor_tensor(ra[:], ry[:], ry[:], ALU.mult))
                    settle()
                    put(dve.scalar_tensor_tensor(out=rb[:], in0=ra[:], scalar=-0.5, in1=rv[:], op0=ALU.mult, op1=ALU.mult))
                    settle()
                    put(dve.scalar_tensor_tensor(out=ry[:], in0=rb[:], scalar=1.5, in1=ry[:], op0=ALU.add, op1=ALU.mult))
                    settle()
                for t in range(GT):
                    ins = dve.tensor_scalar(dst[:, t, :], src[:, t, :], mv[:, t, 0:1], ry[:, t:t + 1], ALU.subtract, ALU.mult)
                    if t < GT - 1:
                        put(ins)
                    else:
                        ins.then_inc(done, 1)

            def embed(g):
                t0, par = g * GT, g % 2
                dve.wait_ge(g_emb[g], 16 * 3 * GT)
                if t0 % TB == 0:
                    for j in range(3):
                        put(dve.memset(emb[0:j + 1, t0, j, :], 0.0))
                    settle()
                put(dve.tensor_tensor(tsum[:, par], emb[:, t0:t0 + GT, 0, :], emb[:, t0:t0 + GT, 1, :], ALU.add))
                settle()
                put(dve.tensor_tensor(tsum[:, par], tsum[:, par], emb[:, t0:t0 + GT, 2, :], ALU.add))
                settle()
                layernorm(tsum[:, par], xln[:, par], 16 * EPS, d_xln)
                dve.wait_ge(d_xln, g + 1)
                put(dve.scalar_tensor_tensor(out=h2[:, t0:t0 + GT, :], in0=tsum[:, par], scalar=0.25, in1=xln[:, par],
                                             op0=ALU.mult, op1=ALU.add))

            def causal(g):
                dve.wait_ge(p_sc, g + 1)
                if g:
                    dve.wait_ge(p_retr, g)
                dve.tensor_tensor(pt[:], sc[:], bc_mid(mask, [P, GT, P]), ALU.mult).then_inc(d_mask, 1)

            def state(g):
                dve.wait_ge(p_st, g + 1)
                for t in range(GT):
                    n = g * GT + t
                    if n + 1 == NT:
                        continue
                    new, old = st[:, (n + 1) % (2 * GT), :], st[:, n % (2 * GT), :]
                    if n % TB == 0:
                        ins = dve.tensor_copy(new, ws[:, 1, t, :])
                    else:
                        dve.wait_ge(d_state, n)
                        ins = dve.tensor_tensor(new, ws[:, 1, t, :], old, ALU.add)
                    ins.then_inc(d_state, 1)

            def norm_retrieved(g):
                dve.wait_ge(p_retr, g + 1)
                if g:
                    dve.wait_ge(p_nT, g)
                t0 = g * GT % TB
                layernorm(vr[:, 1], nrm, cw[:, C_EPS + t0:C_EPS + t0 + GT], d_nrm)

            def reduce_phase(g):
                dve.wait_ge(a_tk, g + 1)
                dve.wait_ge(a_tq, g + 1)
                put(dve.tensor_scalar(pu[:], ph[:], cw[:, C_FREQ:C_FREQ + 1], cw[:, C_OFF:C_OFF + 1], ALU.mult, ALU.add))
                settle()
                if g:
                    dve.wait_ge(a_sin, g)
                put(dve.tensor_scalar(pr[:], pu[:], ROUND, ROUND, ALU.add, ALU.subtract))
                settle()
                dve.tensor_tensor(pr[:], pu[:], pr[:], ALU.subtract).then_inc(d_phase, 1)

            def residual(g):
                t0 = g * GT
                dve.wait_ge(p_wo, g + 1)
                put(dve.tensor_tensor(h2[:, t0:t0 + GT, :], h2[:, t0:t0 + GT, :], ws[:, 0], ALU.add))
                settle()
                layernorm(h2[:, t0:t0 + GT, :], pay[:, t0:t0 + GT, 0:D], EPS, d_xf)

            def column(level):
                return {7: 7, 6: 8}.get(level, level)

            def walk(g):
                t0 = g * GT
                dve.wait_ge(p_tree, g + 1)
                put(dve.tensor_copy(lg[:, :, 0], tree[:, :, 0]))
                put(dve.tensor_scalar(cur[:], tree[:, :, 0], 0.0, None, ALU.is_gt))
                settle()
                for level in range(1, LEVELS):
                    w = 1 << level
                    nodes_l = tree[:, :, w - 1:2 * w - 1]
                    col = column(level)
                    if level < LEVELS - 1:
                        m = one[:, t0:t0 + GT, :] if level == LEVELS - 2 else msk[:, :, 0:w]
                        put(dve.tensor_scalar(cur2[:], cur[:], 2.0, None, ALU.mult))
                        put(dve.tensor_tensor(m, bc_mid(iota[:, 0:w], [P, GT, w]), bc(cur[:], [P, GT, w]), ALU.is_equal))
                        settle()
                        put(dve.tensor_tensor(mks[:, :, 0:w], nodes_l, m, ALU.mult))
                        settle()
                        put(dve.tensor_reduce(lg[:, :, col], mks[:, :, 0:w], AXX, ALU.add))
                        settle()
                        put(dve.scalar_tensor_tensor(out=cur[:], in0=lg[:, :, col], scalar=0.0, in1=cur2[:],
                                                     op0=ALU.is_gt, op1=ALU.add))
                        settle()
                    else:
                        put(dve.tensor_scalar(rgt[:], lg[:, :, column(level - 1)], 0.0, None, ALU.is_gt))
                        for t in range(GT):
                            put(dve.scalar_tensor_tensor(out=mks[:, t, 0:w], in0=iota[:, 0:w], scalar=cur[:, t:t + 1],
                                                         in1=nodes_l[:, t, :], op0=ALU.is_equal, op1=ALU.mult,
                                                         accum_out=lg[:, t, col:col + 1]))
                        settle()
                ins = dve.tensor_tensor(mks[:, :, 0], lg[:, :, 7], rgt[:], ALU.mult)
                ins.then_inc(d_one, 1)
                dve.wait_ge(d_one, g + 1)
                put(dve.tensor_tensor(lg[:, :, 6], lg[:, :, 7], mks[:, :, 0], ALU.subtract))
                settle()
                put(dve.tensor_copy(lg[:, :, 7], mks[:, :, 0]))
                settle()
                if g >= 2:
                    dve.wait_ge(a_w, g - 1)
                dve.scalar_tensor_tensor(out=la[:, g % 2], in0=lg[:], scalar=-1.0, in1=lg[:],
                                         op0=ALU.mult, op1=ALU.max).then_inc(d_walk, 1)

            def place(g):
                t0 = g * GT
                dve.wait_ge(p_rank, g + 1)
                prk = tree[:, 0, :].rearrange("p (t w) -> p t w", t=GT)
                put(dve.tensor_tensor(rtmp[:], prk, one[:, t0:t0 + GT, :], ALU.mult))
                put(dve.tensor_tensor(lpart[:], one[:, t0, :], one[:, t0 + 1, :], ALU.add))
                settle()
                put(dve.tensor_reduce(rank[:, t0:t0 + GT], rtmp[:], AXX, ALU.add))
                put(dve.tensor_tensor(lpart[:], lpart[:], one[:, t0 + 2, :], ALU.add))
                settle()
                put(dve.tensor_tensor(rtmp[:], bc_mid(iota[:, 0:PAR], [P, GT, PAR]), one[:, t0:t0 + GT, :], ALU.mult))
                put(dve.tensor_tensor(lpart[:], lpart[:], one[:, t0 + 3, :], ALU.add))
                settle()
                put(dve.tensor_reduce(far[:], rtmp[:], AXX, ALU.add))
                dve.tensor_tensor(lsum[:], lsum[:], lpart[:], ALU.add).then_inc(d_rank, 1)
                settle()
                put(dve.scalar_tensor_tensor(out=row0[:, t0:t0 + GT], in0=rank[:, t0:t0 + GT], scalar=float(PAR), in1=far[:],
                                             op0=ALU.mult, op1=ALU.add))
                settle()
                put(dve.tensor_scalar(far[:], rank[:, t0:t0 + GT], float(P), float(FAR), ALU.is_ge, ALU.mult))
                settle()
                dve.tensor_tensor(idx1[:, t0:t0 + GT], row0[:, t0:t0 + GT], far[:], ALU.add).then_inc(d_slot, 1)

            for k in range(NG + 2):
                if k < NG:
                    embed(k)
                if 1 <= k <= NG:
                    causal(k - 1)
                if k >= 2:
                    walk(k - 2)
                if 1 <= k <= NG:
                    state(k - 1)
                    norm_retrieved(k - 1)
                if k < NG:
                    reduce_phase(k)
                if k >= 2:
                    place(k - 2)
                if 1 <= k <= NG:
                    residual(k - 1)

            dve.wait_ge(p_cnt, 1)
            put(dve.tensor_scalar(ovi[:], vr[:, 0, 0, :], float(P - 1), None, ALU.add))
            put(dve.tensor_scalar(oci[:], vr[0:PAR, 0, 1, 0:1], float(P - 1), None, ALU.add))
            settle()
            put(dve.tensor_single_scalar(ovi[:], ovi[:], 7, op=ALU.logical_shift_right))
            put(dve.tensor_single_scalar(oci[:], oci[:], 7, op=ALU.logical_shift_right))
            settle()
            dve.tensor_scalar(oce[:], oci[:], -1.0, 0.0, ALU.add, ALU.max).then_inc(d_ovc, 1)
            put(dve.tensor_scalar(ovr[:], ovi[:], -1.0, 0.0, ALU.add, ALU.max))
            settle()
            put(dve.tensor_tensor_scan(ovinc[:], onesf[:], ovr[:], 0.0, ALU.mult, ALU.add))
            settle()
            put(dve.tensor_tensor(ovexc[:], ovinc[:], ovr[:], ALU.subtract))
            dve.wait_ge(p_ovi, 1)
            put(dve.tensor_copy(occ[:], vr[0:PAR, 0, 1, 1:2]))
            settle()
            dve.tensor_scalar(cmp[:], iota[0:PAR, 0:OVP], occ[:], None, ALU.is_ge).then_inc(d_cmp, 1)
            put(dve.tensor_scalar(pgi[0:1, OVP:OVP + 1], ovinc[0:1, PAR - 1:PAR], 1.0, None, ALU.max))
            dve.wait_ge(p_pg, 1)
            dve.tensor_scalar(pgi[0:1, 0:OVP], vr[0:1, 0, 2, 0:OVP], float(PAR - 1), None, ALU.min).then_inc(d_pg, 1)
            tmp = ys[:].rearrange("p a d -> p (a d)")[:, 0:NT * PAR].rearrange("p (t w) -> p t w", t=NT)
            put(dve.tensor_tensor(tmp, one[:], bc_mid(ovexc[:], [P, NT, PAR]), ALU.mult))
            put(dve.tensor_copy(tki[:], rank[:]))
            settle()
            put(dve.tensor_reduce(tk[:, 0, :], tmp, AXX, ALU.add))
            put(dve.tensor_single_scalar(tki[:], tki[:], 7, op=ALU.logical_shift_right))
            put(dve.tensor_scalar(tk[:, 5, :], rank[:], float(P), None, ALU.is_ge))
            settle()
            put(dve.tensor_copy(tk[:, 1, :], tki[:]))
            settle()
            put(dve.scalar_tensor_tensor(out=tk[:, 2, :], in0=tk[:, 1, :], scalar=float(1 - P * OVP), in1=tk[:, 0, :],
                                         op0=ALU.mult, op1=ALU.add))
            settle()
            put(dve.scalar_tensor_tensor(out=tk[:, 3, :], in0=rank[:], scalar=float(OVP), in1=tk[:, 2, :],
                                         op0=ALU.mult, op1=ALU.add))
            settle()
            put(dve.tensor_scalar(tk[:, 3, :], tk[:, 3, :], float(OV0 - 1), None, ALU.add))
            put(dve.tensor_scalar(tk[:, 4, :], tk[:, 5, :], -float(FAR), float(FAR), ALU.mult, ALU.add))
            settle()
            dve.tensor_tensor(idx2[:], tk[:, 3, :], tk[:, 4, :], ALU.add).then_inc(d_idx2, 1)
            put(dve.tensor_tensor(tk[:, 0, :], tk[:, 3, :], row0[:], ALU.subtract))
            settle()
            put(dve.tensor_tensor(tk[:, 0, :], tk[:, 0, :], tk[:, 5, :], ALU.mult))
            settle()
            put(dve.tensor_tensor(idx3[:], tk[:, 0, :], row0[:], ALU.add))
            settle()

            dve.wait_ge(s_clear, 2)

            def products(n, b, src, col, wait_free):
                if wait_free is not None:
                    dve.wait_ge(p_tr, wait_free)
                xcol = src[:, col, 0:D] if isinstance(col, int) else src[:, bass.ds(col, 1), 0:D].rearrange("p a d -> p (a d)")
                gcol = src[:, col, D:PW] if isinstance(col, int) else src[:, bass.ds(col, 1), D:PW].rearrange("p a d -> p (a d)")
                zx = z[:, b, 0:9 * D].rearrange("p (a d) -> p a d", d=D)
                dve.tensor_tensor(zx, bc_mid(xcol, [P, 9, D]), bc(gcol, [P, 9, D]), ALU.mult)
                dve.tensor_scalar(z[:, b, 9 * D:9 * D + 9], gcol, 1.0, None, ALU.mult).then_inc(d_z, 1)

            yps = [vr[:, 1, 0, :], ws[:, 0, 0, :]]

            def result(n, b, dst, col):
                dve.wait_ge(p_mm, n + 1)
                d = dst[:, col, :] if isinstance(col, int) else dst[:, bass.ds(col, 1), :].rearrange("p a d -> p (a d)")
                dve.tensor_scalar(d, yps[b], 1.0, None, ALU.mult).then_inc(d_y, 1)

            dve.wait_ge(s_xs, 16)
            products(0, 0, xs, 0, None)
            products(1, 1, xs, 1, None)
            with dve.Fori(1, PAR // 2) as i:
                dve.wait_ge(s_xs, (i >> 2) * 16 + 16)
                products(i * 2, 0, xs, i * 2, i * 2 - 1)
                result(i * 2 - 2, 0, ys, i * 2 - 2)
                products(i * 2 + 1, 1, xs, i * 2 + 1, i * 2)
                result(i * 2 - 1, 1, ys, i * 2 - 1)
            result(PAR - 2, 0, ys, PAR - 2)
            result(PAR - 1, 1, ys, PAR - 1)
            dve.wait_ge(s_xov, 16)
            npg = dve.value_load(pgi[0:1, OVP:OVP + 1], min_val=1, max_val=OVP)
            with dve.Fori(0, npg) as j:
                products(None, 0, xov, j, j + PAR)
                result(j + PAR, 0, yov, j)

            for g in range(NG):
                dve.wait_ge(g_y[g], 16 * GT)
                t0 = g * GT
                dve.tensor_tensor(yg[:, t0:t0 + GT, :], yg[:, t0:t0 + GT, :], h2[:, t0:t0 + GT, :], ALU.add).then_inc(d_out, 1)


def lay_out_small(np, w):
    a = np.zeros((P, C_ALL), np.float32)
    r = np.arange(P)
    a[:, C_ID:C_ID + P] = r[:, None] == r[None]
    a[:, C_MASK:C_MASK + P] = r[:, None] <= r[None]
    a[:, C_IOTA:C_IOTA + P] = r[None]
    a[:, C_FREQ] = 2.0 ** (r % K // 16) / 2
    a[:, C_OFF] = np.where(r < K, 0.25, 0.0)
    a[:, C_EPS:C_EPS + TB] = EPS * K * (1 + r[:, None] + P * np.arange(TB)[None])
    a[:D, C_W1:C_W1 + D], a[:D, C_W1 + D:C_W1 + P] = w["Wk1"], w["Wq1"]
    for n in range(2):
        a[:D, C_W2 + n * K:C_W2 + (n + 1) * K] = w["Wk2"]
        a[D:, C_W2 + n * K:C_W2 + (n + 1) * K] = w["Wq2"]
        a[n * K:(n + 1) * K, C_B2K] = w["bk2"]
        a[n * K:(n + 1) * K, C_B2Q] = w["bq2"]
    a[:D, C_B1], a[D:, C_B1] = w["bk1"], w["bq1"]
    a[:D, C_WV:C_WV + D], a[D, C_WV:C_WV + D] = w["Wv"], w["bv"]
    a[:D, C_WO:C_WO + D], a[D, C_WO:C_WO + D] = w["Wo"], w["bo"]
    a[:D, C_TREE:C_TREE + NODES], a[D, C_TREE:C_TREE + NODES] = w["w1s"].T, w["b1s"]
    a[:D, C_LNW], a[D, C_LNW] = w["ln_w"], 1.0
    a[:D, C_LNB], a[D, C_LNB] = w["ln_b"], 1.0
    return a


def lay_out_nodes(np, w2s, b2s):
    a = np.zeros((P, NBLK, D), np.float32)
    for c0, upper, count in ((W01, 0, 2), (W23, 2, 8), (W45, 4, 32)):
        j = np.arange(count)
        a[:D, c0:c0 + count] = w2s[(1 << upper) - 1 + j // 2].transpose(1, 0, 2)
        a[D:, c0:c0 + count] = w2s[(2 << upper) - 1 + j].transpose(1, 0, 2)
    p = np.arange(PAR)
    a[:D, W7:W7 + PAR] = w2s[127 + 2 * p].transpose(1, 0, 2)
    a[D:, W7:W7 + PAR] = w2s[128 + 2 * p].transpose(1, 0, 2)
    a[:D, W6:W6 + PAR] = w2s[63 + p].transpose(1, 0, 2)
    for level in range(6):
        a[D + level, W6:W6 + PAR] = b2s[(1 << level) - 1 + (p >> (6 - level))]
    a[D + 6, W6:W6 + PAR] = b2s[127 + 2 * p]
    a[D + 7, W6:W6 + PAR] = b2s[128 + 2 * p]
    a[D + 8, W6:W6 + PAR] = b2s[63 + p]
    return a.reshape(P, NBLK * D)


def kernel(**inputs):
    import numpy as np
    import concourse.bacc as bacc
    from concourse.bass_utils import run_bass_kernel_spmd as run

    get = lambda name: np.ascontiguousarray(inputs[name])
    w = {n: get(f"L0_attn_{n}") for n in ("Wk1", "bk1", "Wk2", "bk2", "Wq1", "bq1", "Wq2", "bq2", "Wv", "bv", "ln_w", "ln_b", "Wo", "bo")}
    w["w1s"], w["b1s"] = get("L0_ffn_w1s"), get("L0_ffn_b1s")
    arrays = {
        "ids": get("x"), "emb2": get("L0_tok_emb_2"), "emb3": get("L0_tok_emb_3"), "emb4": get("L0_tok_emb_4"),
        "small": lay_out_small(np, w), "nodes": lay_out_nodes(np, get("L0_ffn_w2s"), get("L0_ffn_b2s")),
    }
    nc = bacc.Bacc("TRN2", target_bir_lowering=False, num_devices=1)
    args = [nc.dram_tensor(n, a.shape, mybir.dt.from_np(a.dtype), kind="ExternalInput").ap() for n, a in arrays.items()]
    out = nc.dram_tensor("out", (B, T, D), F32, kind="ExternalOutput").ap()
    build(nc, *args, out)
    return run(nc, [arrays], core_ids=[0]).results[0]["out"]
```

```python
from contextlib import ExitStack

import concourse.bass as bass
from concourse import mybir

F32 = mybir.dt.float32
BF16 = mybir.dt.bfloat16
I32 = mybir.dt.int32
ALU = mybir.AluOpType
ACT = mybir.ActivationFunctionType
AXX = mybir.AxisListType.X

P = 128
B, T, D = 2, 2048, 64
K = 64
VOCAB = 125000
PRIME = 31
EPS = 1e-5
NT = B * T // P
TB = T // P
GT = 4
NG = NT // GT
GN = GT * P
NODES = 255
LEVELS = 8
PAR = 64
NW = 9
GW = 32
PW = D + GW // 2
CH = 8
OVP = 32
SLOTS = (PAR + OVP) * P
OV0 = PAR * P
FAR = 1 << 16
TWO_PI = 6.283185
ROUND = 12582912.0
W01, W23, W45, W7, W6 = 0, 2, 10, 42, 106
NBLK = 170

COLUMNS = [("ID", P), ("MASK", P), ("IOTA", P), ("FREQ", 1), ("OFF", 1), ("EPS", NG // B * 3 * GT), ("W1", P), ("W2", P),
           ("WV", D), ("WO", D), ("TREE", NODES), ("B1", 1), ("B2K", 1), ("B2Q", 1), ("LNW", 1), ("LNB", 1), ("SEL", 5 * P)]
C = {}
C_ALL = 0
for _name, _n in COLUMNS:
    C[_name] = C_ALL
    C_ALL += _n


class Chain:

    def __init__(self, eng, sem):
        self.eng, self.sem, self.n = eng, sem, 0

    def put(self, ins):
        self.n += 1
        ins.then_inc(self.sem, 1)

    def settle(self):
        self.eng.wait_ge(self.sem, self.n)


def build(nc, x, emb2, emb3, emb4, small, nodes, out):
    with ExitStack() as ctx:
        def sb(name, shape, dt=F32):
            return ctx.enter_context(nc.sbuf_tensor(name, shape, dt))

        def psum(name, shape):
            return ctx.enter_context(nc.psum_tensor(name, shape, F32))

        def sem(name):
            return ctx.enter_context(nc.semaphore(name))

        def sems(names):
            return [sem(n) for n in names.split()]

        tp = psum("tp", [P, 512])
        mm = psum("mm", [P, 2, 512])
        vr = psum("vr", [P, 2, GT, D])
        sc = psum("sc", [P, GT, P])
        ws = psum("ws", [P, 2, GT, D])
        tree = psum("tree", [P, GT, 256])

        cw = sb("cw", [P, C_ALL])

        def const(name, rows=P, n=None):
            return cw[0:rows, C[name]:C[name] + (n or dict(COLUMNS)[name])]

        ident, mask, iota = const("ID"), const("MASK"), const("IOTA")
        tri64 = sb("tri64", [P, P], BF16)
        ones64 = sb("ones64", [P, P], BF16)
        onesb = sb("onesb", [P, P], BF16)
        iotab = sb("iotab", [1, PAR], BF16)
        sel = sb("sel", [P, 5, P], BF16)
        lw = sb("lw", [D + 1, D + 1])
        wo_s = sb("wo_s", [D + 1, D])
        xi = sb("xi", [NT, 3 + P], I32)
        xf = sb("xf", [NT, 3 + P])
        hs = sb("hs", [NT, 3, P])
        hq = sb("hq", [NT, 3, P])
        idx = sb("idx", [P, 3, NT], I32)
        emb = sb("emb", [P, NT, 3, D])
        tsum = sb("tsum", [P, 2, GT, D])
        bn = sb("bn", [P, 3 * GT, 6])
        mv = sb("mv", [P, 3 * GT, 2])
        rv, ry, ra, rb = (sb(n, [P, 3 * GT]) for n in ("rv", "ry", "ra", "rb"))
        ri = sb("ri", [P, 3 * GT], I32)
        xln = sb("xln", [P, 2, GT, D])
        h2 = sb("h2", [P, NT, D])
        xT = sb("xT", [D + 1, 2, GN])
        hid = sb("hid", [P, GN])
        ph = sb("ph", [P, 2, GN])
        pu = sb("pu", [P, 2, GN])
        pr = sb("pr", [P, 2, GN])
        feat = sb("feat", [P, 2, 2, GN])
        kft = sb("kft", [P, GT, P])
        vs = sb("vs", [P, 2, GT, D])
        pt = sb("pt", [P, GT, P])
        st = sb("st", [P, 2 * GT, D])
        nrm = sb("nrm", [P, GT, D])
        nT = sb("nT", [D + 1, GN])
        fT = sb("fT", [D + 1, GN])
        pay = sb("pay", [P, NT, PW])
        path = sb("path", [P, GT, 256])
        pscore = sb("pscore", [P, GT, 256])
        lg = sb("lg", [P, GT, NW])
        la = sb("la", [P, 2, GT, NW])
        gw = sb("gw", [P, 2, GT, NW])
        gr = sb("gr", [P, GT, NW])
        one = sb("one", [P, NT, PAR], BF16)
        lsum = sb("lsum", [P, PAR], BF16)
        lpart = sb("lpart", [P, PAR], BF16)
        rtmp = sb("rtmp", [P, GT, PAR])
        row0 = sb("row0", [P, NT])
        far = sb("far", [P, GT])
        idx1 = sb("idx1", [P, NT], I32)
        wf = sb("wf", [P, NBLK, D])
        xs = emb[:].rearrange("p t j d -> p (t j d)")[:, 0:PAR * PW].rearrange("p (a w) -> p a w", w=PW)
        xov = sb("xov", [P, OVP, PW])
        parts = sb("parts", [P, 2, CH * GW], BF16)
        xo1 = sb("xo1", [P, 2, D])
        go1 = sb("go1", [P, GW], BF16)
        x1, xb = (feat[:, n].rearrange("p a (t s) -> p a t s", t=4) for n in range(2))
        gT = sb("gT", [P, 2, P], BF16)
        zT = sb("zT", [P, 2, 5, P])
        ys = sb("ys", [P, PAR, D])
        yov = sb("yov", [P, OVP, D])
        ovr, ovinc, ovexc, onesf = (sb(n, [P, PAR]) for n in ("ovr", "ovinc", "ovexc", "onesf"))
        ovi = sb("ovi", [P, PAR], I32)
        occ = sb("occ", [PAR, 1])
        oci = sb("oci", [PAR, 1], I32)
        oce = sb("oce", [PAR, 1])
        cmp = sb("cmp", [PAR, OVP])
        pgi = sb("pgi", [1, OVP + 1], I32)
        tk = sb("tk", [P, 5, NT])
        tki = sb("tki", [P, 3, NT], I32)
        idx2 = sb("idx2", [P, NT], I32)
        idx3 = sb("idx3", [P, NT], I32)
        yg = pay[:].rearrange("p t w -> p (t w)")[:, 0:NT * D].rearrange("p (t d) -> p t d", d=D)

        slots = nc.dram_tensor("slots", (SLOTS, PW), F32, kind="Internal").ap()
        ydram = nc.dram_tensor("ydram", (SLOTS, D), F32, kind="Internal").ap()

        s_ids, s_ident, s_small, s_wf, s_slot0 = sems("s_ids s_ident s_small s_wf s_slot0")
        g_clear, dv = sems("g_clear dv")
        d_hash, p_hash, d_idx, d_lw, p_lw, d_wo, d_ones = sems("d_hash p_hash d_idx d_lw p_lw d_wo d_ones")
        g_emb = [sem(f"g_emb{g}") for g in range(NG)]
        g_scat = [sem(f"g_scat{g}") for g in range(NG)]
        d_xln, d_phase, d_mask, d_state, d_res, d_nrm, d_xf = sems("d_xln d_phase d_mask d_state d_res d_nrm d_xf")
        d_one, d_read, d_walk, d_rank, d_slot, d_pay = sems("d_one d_read d_walk d_rank d_slot d_pay")
        p_xT, p_hid, p_v, p_sc, p_phk, p_phq, p_retr, p_st = sems("p_xT p_hid p_v p_sc p_phk p_phq p_retr p_st")
        p_nT, p_wo, p_kft, p_fT, p_tree, p_rank = sems("p_nT p_wo p_kft p_fT p_tree p_rank")
        a_xT, a_hid, a_v, a_tk, a_tq, a_w, a_nT, a_sin, a_kft, a_fT = sems("a_xT a_hid a_v a_tk a_tq a_w a_nT a_sin a_kft a_fT")
        p_cnt, d_ovc, p_ovi, d_cmp, p_pg, d_pg, d_idx2 = sems("p_cnt d_ovc p_ovi d_cmp p_pg d_pg d_idx2")
        g_second, s_xs, s_xov, d_parts = sems("g_second s_xs s_xov d_parts")
        p_gt, a_gt, p_x, a_x, p_g, d_z, p_mm, a_y = sems("p_gt a_gt p_x a_x p_g d_z p_mm a_y")
        d_ov, p_ov, a_ov, d_yov = sems("d_ov p_ov a_ov d_yov")
        s_y, s_yov, s_stored = sems("s_y s_yov s_stored")
        g_y = [sem(f"g_y{g}") for g in range(NG)]
        d_out, s_out = sems("d_out s_out")

        def bc_mid(ap, shape):
            return ap.unsqueeze(1).to_broadcast(shape)

        def tile(t):
            return slice(t * P, (t + 1) * P)

        def tiles(g):
            return slice(g * GT, (g + 1) * GT)

        ids = x.rearrange("b t -> (b t)")
        gps = [tree[:].rearrange("p a b -> p (a b)"), mm[:].rearrange("p a b -> p (a b)")]
        gtp = sc[:].rearrange("p a b -> p (a b)").bitcast(BF16)[:, 0:P]
        yps = [vr[:, 0], ws[:, 0]]

        block = ctx.enter_context(nc.Block())

        @block.sync
        def _(sp):
            rows = ids.rearrange("(n p) -> n p", p=P)
            sp.dma_start(xi[0:NT, 3:3 + P], rows).then_inc(s_ids, 16)
            sp.dma_start(xi[1:NT, 0:3], rows[0:NT - 1, P - 3:P]).then_inc(s_ids, 16)
            sp.dma_start(cw[:, 0:P], small[:, 0:P]).then_inc(s_ident, 16)
            sp.dma_start(cw[:, P:C_ALL], small[:, P:C_ALL]).then_inc(s_small, 16)
            flat = slots.rearrange("(q a) d -> q (a d)", q=P)
            width, zero = SLOTS // P * PW, yov[:].rearrange("p a d -> p (a d)")
            pieces = [(c0, min(OVP * D, width - c0)) for c0 in range(0, width, OVP * D)]
            sp.wait_ge(g_clear, 1)
            assert len(pieces) == 4
            quarter = (NBLK + 3) // 4
            for n, (c0, w) in enumerate(pieces):
                sp.wait_ge(g_emb[n], 16 * 3 * GT)
                sp.dma_start(flat[:, c0:c0 + w], zero[:, 0:w]).then_inc(s_slot0, 16)
                if n == 0:
                    sp.dma_start(ydram[OV0:SLOTS].rearrange("(q a) d -> q a d", q=P), yov[:]).then_inc(s_slot0, 16)
            for n in range(4):
                b0, b1 = n * quarter, min(NBLK, (n + 1) * quarter)
                sp.wait_ge(g_emb[n + 4], 16 * 3 * GT)
                sp.dma_start(wf[:, b0:b1, :].rearrange("p b d -> p (b d)"), nodes[:, b0 * D:b1 * D]).then_inc(s_wf, 16)
            for g in range(NG):
                sp.wait_ge(g_scat[g], 16 * GT)
            page = slots[0:OV0].rearrange("(q a) d -> q a d", q=P)
            for c in range(PAR // CH):
                if c:
                    sp.wait_ge(s_xs, 16 * c)
                sp.dma_start(xs[:, c * CH:(c + 1) * CH, :], page[:, c * CH:(c + 1) * CH, :]).then_inc(s_xs, 16)
            sp.wait_ge(g_second, 16 * NT)
            sp.dma_start(xov[:], slots[OV0:SLOTS].rearrange("(q a) d -> q a d", q=P)).then_inc(s_xov, 16)
            ypage = ydram[0:OV0].rearrange("(q a) d -> q a d", q=P)
            for c in range(PAR // CH):
                sp.wait_ge(a_y, (c + 1) * CH // 4)
                sp.dma_start(ypage[:, c * CH:(c + 1) * CH, :], ys[:, c * CH:(c + 1) * CH, :]).then_inc(s_y, 16)
            yo = ydram[OV0:SLOTS].rearrange("(q a) d -> q a d", q=P)
            npg = sp.value_load(pgi[0:1, OVP:OVP + 1], min_val=1, max_val=OVP)
            with sp.Fori(0, npg) as j:
                sp.wait_ge(d_yov, j + 1)
                sp.dma_start(yo[:, bass.ds(j, 1), :], yov[:, bass.ds(j, 1), :]).then_inc(s_yov, 16)
            sp.wait_ge(s_y, 16 * (PAR // CH))
            sp.wait_ge(s_yov, npg * 16)
            sp.sem_inc(s_stored, 1)
            for g in range(NG):
                sp.wait_ge(d_out, g + 1)
                b, t0 = divmod(g * GT, TB)
                sp.dma_start(out[b].rearrange("(t p) d -> p t d", p=P)[:, t0:t0 + GT, :],
                             yg[:, tiles(g), :]).then_inc(s_out, 16)
            sp.wait_ge(s_out, 16 * NG)

        @block.gpsimd
        def _(pool):
            pool.memset(yov[:], 0.0).then_inc(g_clear, 1)
            pool.memset(pay[:, :, D:PW], 0.0).then_inc(g_clear, 1)

            def gather(g):
                for t in range(g * GT, (g + 1) * GT):
                    for j, table in enumerate((emb2, emb3, emb4)):
                        pool.indirect_dma_start(emb[:, t, j, :], None, table,
                                                bass.IndirectOffsetOnAxis(idx[:, j, t:t + 1], 0)).then_inc(g_emb[g], 16)

            def scatter(g):
                pool.wait_ge(d_slot, g + 1)
                pool.wait_ge(d_pay, g + 1)
                for t in range(g * GT, (g + 1) * GT):
                    pool.indirect_dma_start(slots, bass.IndirectOffsetOnAxis(idx1[:, t:t + 1], 0), pay[:, t, :], None,
                                            bounds_check=SLOTS - 1, oob_is_err=False).then_inc(g_scat[g], 16)

            pool.wait_ge(d_idx, 1)
            AHEAD = 6
            for g in range(NG + AHEAD):
                if g < NG:
                    gather(g)
                if g == AHEAD - 1:
                    pool.wait_ge(s_slot0, 80)
                if g >= AHEAD - 1 and g - AHEAD + 1 < NG:
                    scatter(g - AHEAD + 1)
            pool.wait_ge(d_idx2, 1)
            for t in range(NT):
                pool.indirect_dma_start(slots, bass.IndirectOffsetOnAxis(idx2[:, t:t + 1], 0), pay[:, t, :], None,
                                        bounds_check=SLOTS - 1, oob_is_err=False).then_inc(g_second, 16)
            pool.wait_ge(g_second, 16 * NT)
            pool.wait_ge(s_stored, 1)
            for t in range(NT):
                pool.indirect_dma_start(yg[:, t, :], None, ydram,
                                        bass.IndirectOffsetOnAxis(idx3[:, t:t + 1], 0)).then_inc(g_y[t // GT], 16)

        @block.scalar
        def _(act):
            act.wait_ge(s_small, 16)
            act.wait_ge(d_ones, 1)

            def encode(g):
                act.wait_ge(p_xT, g + 1)
                act.copy(xT[0:D, g % 2, :], tp[0:D, :]).then_inc(a_xT, 1)
                act.wait_ge(p_hid, g + 1)
                act.activation(hid[:], mm[:, 0, :], ACT.Gelu, bias=const("B1")).then_inc(a_hid, 1)

            def turn_nrm(g):
                act.wait_ge(p_nT, g + 1)
                act.copy(nT[0:D, :], tp[0:D, :]).then_inc(a_nT, 1)

            def phases(g):
                act.wait_ge(p_v, g + 1)
                act.copy(vs[:, g % 2], vr[:, 0]).then_inc(a_v, 1)
                act.wait_ge(p_phk, g + 1)
                act.activation(ph[:, 0, :], mm[:, 1, :], ACT.Tanh, bias=const("B2K")).then_inc(a_tk, 1)
                act.wait_ge(p_phq, g + 1)
                act.activation(ph[:, 1, :], mm[:, 0, :], ACT.Tanh, bias=const("B2Q")).then_inc(a_tq, 1)

            def turn_xf(g):
                act.wait_ge(p_fT, g + 1)
                act.copy(fT[0:D, :], tp[0:D, :]).then_inc(a_fT, 1)

            def features(g):
                act.wait_ge(d_phase, g + 1)
                act.activation(feat[:, g % 2], pr[:], ACT.Sin, scale=TWO_PI).then_inc(a_sin, 1)
                act.wait_ge(p_kft, g + 1)
                act.copy(kft[:], mm[:, 1, :].rearrange("p (t f) -> p t f", t=GT)).then_inc(a_kft, 1)

            def weights(g):
                act.wait_ge(d_walk, g + 1)
                act.activation(gw[:, g % 2], la[:, g % 2], ACT.Gelu).then_inc(a_w, 1)

            for k in range(NG + 3):
                if k < NG:
                    encode(k)
                if 0 <= k - 1 < NG:
                    turn_nrm(k - 1)
                if k < NG:
                    phases(k)
                if 0 <= k - 2 < NG:
                    turn_xf(k - 2)
                if k < NG:
                    features(k)
                if 0 <= k - 3 < NG:
                    weights(k - 3)

            def turn_weights(q):
                act.wait_ge(p_gt, q + 1)
                act.copy(gT[:, q % 2, :], gtp).then_inc(a_gt, 1)

            def turn_pages(q):
                act.wait_ge(p_x, q + 1)
                if q >= 2:
                    act.wait_ge(d_z, 4 * q - 4)
                xT4 = tp[0:D, :].rearrange("p (a b) -> p a b", a=4)
                act.copy(x1[0:D, q % 2], xT4)
                act.copy(x1[D:P, q % 2], xT4)
                act.copy(xb[0:D, q % 2], xT4).then_inc(a_x, 1)

            def results(q):
                act.wait_ge(p_mm, 4 * q + 4)
                act.copy(ys[:, 4 * q:4 * q + 4, :], yps[q % 2]).then_inc(a_y, 1)

            turn_weights(0)
            turn_pages(0)
            for n in range(PAR):
                if n % 4 == 0 and n + 4 < PAR:
                    turn_weights(n // 4 + 1)
                    turn_pages(n // 4 + 1)
                if n % 4 == 1 and n > 4:
                    results(n // 4 - 1)
            results(PAR // 4 - 1)
            npg = act.value_load(pgi[0:1, OVP:OVP + 1], min_val=1, max_val=OVP)
            with act.Fori(0, npg) as j:
                act.wait_ge(p_ov, j + 1)
                act.copy(gT[0:GW, 0, :], gtp[0:GW, :])
                act.copy(x1[:, 0, 0, :], tp[:, 0:P])
                act.copy(xb[0:D, 0, 0, :], tp[0:D, 0:P]).then_inc(a_ov, 1)

        @block.tensor
        def _(pe):
            wv, wtree = const("WV", D + 1), const("TREE", D + 1)

            pe.wait_ge(s_ident, 16)
            pe.wait_ge(d_hash, 1)
            for j in range(3):
                last = pe.transpose(tp[:, j * NT:(j + 1) * NT], hs[:, j, :], ident[0:NT, 0:NT])
            last.then_inc(p_hash, 1)
            pe.wait_ge(d_lw, 1)
            pe.matmul(ws[0:D + 1, 0, 0, :], lw[:], const("WO", D + 1), start=True, stop=True).then_inc(p_lw, 1)

            def attend(g):
                pe.wait_ge(a_kft, g + 1)
                pe.wait_ge(a_v, g + 1)
                pe.wait_ge(d_res, g) if g else pe.wait_ge(d_wo, 1)
                for t in range(GT):
                    last = pe.matmul(ws[:, 1, t, :], kft[:, t, :], vs[:, g % 2, t, :], start=True, stop=True)
                last.then_inc(p_st, 1)
                pe.wait_ge(d_mask, g + 1)
                for t in range(GT):
                    n = g * GT + t
                    first = n % TB == 0
                    last = pe.matmul(vr[:, 1, t, :], pt[:, t, :], vs[:, g % 2, t, :], start=True, stop=first)
                    if not first:
                        pe.wait_ge(d_state, n)
                        last = pe.matmul(vr[:, 1, t, :], feat[:, g % 2, 1, tile(t)], st[:, n % (2 * GT), :],
                                         start=False, stop=True)
                last.then_inc(p_retr, 1)

            def turn_x(g):
                pe.wait_ge(d_xln, g + 1)
                if g >= 3:
                    pe.wait_ge(a_fT, g - 2)
                elif g == 0:
                    pe.wait_ge(d_idx, 1)
                for t in range(GT):
                    last = pe.transpose(tp[0:D, tile(t)], xln[:, g % 2, t, :], ident)
                last.then_inc(p_xT, 1)

            def hidden(g):
                pe.wait_ge(a_xT, g + 1)
                if g >= 4:
                    pe.wait_ge(d_rank, g - 3)
                pe.matmul(mm[:, 0, :], const("W1", D), xT[0:D, g % 2, :], start=True, stop=True).then_inc(p_hid, 1)

            def turn_nrm(g):
                pe.wait_ge(d_nrm, g + 1)
                pe.wait_ge(a_xT, min(g + 2, NG))
                for t in range(GT):
                    last = pe.transpose(tp[0:D, tile(t)], nrm[:, t, :], ident)
                last.then_inc(p_nT, 1)

            def phases(g):
                for t in range(GT):
                    last = pe.matmul(vr[:, 0, t, :], xT[:, g % 2, tile(t)], wv, start=True, stop=True)
                last.then_inc(p_v, 1)
                pe.wait_ge(a_hid, g + 1)
                pe.matmul(mm[:, 1, :], const("W2", D), hid[0:D, :], start=True, stop=True).then_inc(p_phk, 1)
                pe.matmul(mm[:, 0, :], cw[D:P, C["W2"]:C["W2"] + P], hid[D:P, :], start=True, stop=True).then_inc(p_phq, 1)

            def project(g):
                pe.wait_ge(a_nT, g + 1)
                pe.wait_ge(d_state, min(GT * (g + 1), NT - 1))
                for t in range(GT):
                    last = pe.matmul(ws[:, 0, t, :], nT[:, tile(t)], wo_s[:], start=True, stop=True)
                last.then_inc(p_wo, 1)

            def turn_xf(g):
                pe.wait_ge(d_xf, g + 1)
                pe.wait_ge(a_nT, min(g + 2, NG))
                for t in range(GT):
                    last = pe.transpose(tp[0:D, tile(t)], pay[:, g * GT + t, 0:D], ident)
                last.then_inc(p_fT, 1)

            def ranks(g):
                pe.wait_ge(d_one, g + 1)
                pe.wait_ge(a_tq, min(g + 4, NG))
                if g:
                    pe.wait_ge(d_rank, g)
                for t in range(GT):
                    parts = [(tri64[:], one[:, g * GT + t, :]), (onesb[0:1, :], iotab[:])]
                    parts += [(ones64[:], one[:, g * GT + u, :]) for u in range(t)]
                    if g:
                        parts.append((ones64[:], lsum[:]))
                    for n, (a, b) in enumerate(parts):
                        last = pe.matmul(mm[:, 0, t * PAR:(t + 1) * PAR], a, b, start=(n == 0), stop=(n == len(parts) - 1))
                last.then_inc(p_rank, 1)

            def scores(g):
                pe.wait_ge(a_sin, g + 1)
                for t in range(GT):
                    last = pe.transpose(mm[:, 1, tile(t)], feat[:, g % 2, 0, tile(t)], ident)
                last.then_inc(p_kft, 1)
                if g:
                    pe.wait_ge(d_mask, g)
                for t in range(GT):
                    last = pe.matmul(sc[:, t, :], feat[:, g % 2, 0, tile(t)], feat[:, g % 2, 1, tile(t)], start=True, stop=True)
                last.then_inc(p_sc, 1)

            def node_scores(g):
                pe.wait_ge(a_fT, g + 1)
                if g:
                    pe.wait_ge(d_read, g)
                for t in range(GT):
                    last = pe.matmul(tree[:, t, 0:NODES], fT[:, tile(t)], wtree, start=True, stop=True)
                last.then_inc(p_tree, 1)

            pe.wait_ge(s_small, 16)
            for k in range(NG + 3):
                if 0 <= k - 1 < NG:
                    attend(k - 1)
                if k < NG:
                    turn_x(k)
                    hidden(k)
                if 0 <= k - 1 < NG:
                    turn_nrm(k - 1)
                if k < NG:
                    phases(k)
                if 0 <= k - 1 < NG:
                    project(k - 1)
                if 0 <= k - 2 < NG:
                    turn_xf(k - 2)
                if 0 <= k - 3 < NG:
                    ranks(k - 3)
                if k < NG:
                    scores(k)
                if 0 <= k - 2 < NG:
                    node_scores(k - 2)

            pe.wait_ge(d_slot, NG)
            pe.matmul(vr[:, 0, 0, :], onesb[:], lsum[:], start=True, stop=True)
            pe.matmul(vr[0:PAR, 0, 1, 0:1], lsum[:], onesb[:, 0:1], start=True, stop=True).then_inc(p_cnt, 1)
            pe.wait_ge(d_ovc, 1)
            pe.matmul(vr[0:PAR, 0, 1, 1:2], cw[0:PAR, C["MASK"]:C["MASK"] + PAR], oce[:], start=True, stop=True).then_inc(p_ovi, 1)
            pe.wait_ge(d_cmp, 1)
            pe.matmul(vr[0:1, 0, 2, 0:OVP], onesf[0:PAR, 0:1], cmp[:], start=True, stop=True).then_inc(p_pg, 1)

            identb = onesb[:]

            def turn_weights(q):
                if q:
                    pe.wait_ge(a_gt, q)
                pe.wait_ge(d_parts, 4 * q // CH + 1)
                c = 4 * q % CH * GW
                pe.transpose(gtp, parts[:, 4 * q // CH % 2, c:c + 4 * GW], identb).then_inc(p_gt, 1)

            def turn_pages(q):
                if q:
                    pe.wait_ge(a_x, q)
                pe.wait_ge(s_xs, 16 * (4 * q // CH + 1))
                for n in range(4):
                    last = pe.transpose(tp[0:D, tile(n)], xs[:, 4 * q + n, 0:D], ident)
                last.then_inc(p_x, 1)

            def spread(n):
                pe.wait_ge(a_gt, n // 4 + 1)
                if n > 1:
                    pe.wait_ge(d_z, n - 1)
                u = slice(n % 4 * GW, (n % 4 + 1) * GW)
                for c in range(5):
                    last = pe.matmul(gps[n % 2][:, tile(c)], sel[u, c, :], gT[u, n // 4 % 2, :], start=True, stop=True)
                last.then_inc(p_g, 1)

            def node_products(n):
                pe.wait_ge(d_z, n + 1)
                if n % 4 == 0 and n >= 8:
                    pe.wait_ge(a_y, n // 4 - 1)
                for c, blk in enumerate((W01 + (n >> 5), W23 + (n >> 3), W45 + (n >> 1), W7 + n, W6 + n)):
                    rows = P if c < 4 else D + NW
                    last = pe.matmul(yps[n // 4 % 2][:, n % 4, :], zT[0:rows, n % 2, c, :], wf[0:rows, blk, :],
                                     start=(c == 0), stop=(c == 4))
                last.then_inc(p_mm, 1)

            pe.wait_ge(s_wf, 64)
            pe.wait_ge(d_pg, 1)
            turn_weights(0)
            turn_pages(0)
            spread(0)
            for n in range(PAR):
                if n % 4 == 0 and n + 4 < PAR:
                    turn_weights(n // 4 + 1)
                    turn_pages(n // 4 + 1)
                if n + 1 < PAR:
                    spread(n + 1)
                node_products(n)
            npg = pe.value_load(pgi[0:1, OVP:OVP + 1], min_val=1, max_val=OVP)
            with pe.Fori(0, npg) as j:
                par = pe.value_load(pgi[0:1, bass.ds(j, 1)], min_val=0, max_val=PAR - 1)
                pe.wait_ge(d_ov, j + 1)
                pe.transpose(gtp[0:GW, :], go1[:], identb)
                pe.transpose(tp[:, 0:P], xo1[:].rearrange("p a d -> p (a d)"), ident).then_inc(p_ov, 1)
                pe.wait_ge(a_ov, j + 1)
                for c in range(5):
                    last = pe.matmul(gps[0][:, tile(c)], sel[0:GW, c, :], gT[0:GW, 0, :], start=True, stop=True)
                last.then_inc(p_g, 1)
                pe.wait_ge(d_z, j + (PAR + 1))
                for c, blk in enumerate([(par >> 5) + W01, (par >> 3) + W23, (par >> 1) + W45, par + W7, par + W6]):
                    rows = P if c < 4 else D + NW
                    last = pe.matmul(yps[0][:, 0, :], zT[0:rows, 0, c, :],
                                     wf[0:rows, bass.ds(blk, 1), :].rearrange("p a d -> p (a d)"),
                                     start=(c == 0), stop=(c == 4))
                last.then_inc(p_mm, 1)

        @block.vector
        def _(dve):
            ch = Chain(dve, dv)
            put, settle = ch.put, ch.settle

            put(dve.memset(xi[0:1, 0:3], 0))
            settle()
            dve.wait_ge(s_ids, 32)
            put(dve.tensor_copy(xf[:], xi[:]))
            settle()
            h = hs
            put(dve.scalar_tensor_tensor(out=h[:, 0, :], in0=xf[:, 2:2 + P], scalar=float(PRIME), in1=xf[:, 3:3 + P],
                                         op0=ALU.mult, op1=ALU.add))
            settle()
            put(dve.scalar_tensor_tensor(out=h[:, 1, :], in0=xf[:, 1:1 + P], scalar=float(PRIME ** 2), in1=h[:, 0, :],
                                         op0=ALU.mult, op1=ALU.add))
            settle()
            put(dve.scalar_tensor_tensor(out=h[:, 2, :], in0=xf[:, 0:P], scalar=float(PRIME ** 3), in1=h[:, 1, :],
                                         op0=ALU.mult, op1=ALU.add))
            settle()
            put(dve.tensor_scalar(hq[:], h[:], 1.0 / VOCAB, ROUND, ALU.mult, ALU.add))
            settle()
            put(dve.tensor_scalar(hq[:], hq[:], ROUND, float(VOCAB), ALU.subtract, ALU.mult))
            settle()
            put(dve.tensor_tensor(h[:], h[:], hq[:], ALU.subtract))
            settle()
            put(dve.tensor_scalar(hq[:], h[:], 0.0, float(VOCAB), ALU.is_lt, ALU.mult))
            settle()
            dve.tensor_tensor(h[:], h[:], hq[:], ALU.add).then_inc(d_hash, 1)
            dve.wait_ge(p_hash, 1)
            dve.tensor_copy(idx[:], tp[:, 0:3 * NT].rearrange("p (j t) -> p j t", j=3)).then_inc(d_idx, 1)

            put(dve.memset(xT[D:D + 1, :, :], 1.0))
            put(dve.memset(nT[D:D + 1, :], 1.0))
            dve.memset(fT[D:D + 1, :], 1.0).then_inc(d_ones, 1)
            put(dve.memset(onesb[:], 1.0))
            put(dve.memset(ones64[:], float(PAR)))
            put(dve.memset(onesf[:], 1.0))
            put(dve.memset(lsum[:], 0.0))
            dve.wait_ge(s_small, 16)
            dve.wait_ge(s_ident, 16)
            put(dve.tensor_scalar(lw[:], cw[0:D + 1, 0:D + 1], const("LNW", D + 1), None, ALU.mult))
            settle()
            dve.tensor_copy(lw[:, D:D + 1], const("LNB", D + 1)).then_inc(d_lw, 1)
            put(dve.tensor_tensor(rtmp[:].rearrange("p a b -> p (a b)")[:, 0:P], mask, ident, ALU.subtract))
            put(dve.tensor_copy(iotab[:], iota[0:1, 0:PAR]))
            put(dve.tensor_copy(sel[:].rearrange("p a b -> p (a b)"), const("SEL")))
            settle()
            put(dve.tensor_scalar(tri64[:], rtmp[:].rearrange("p a b -> p (a b)")[:, 0:P], float(PAR), None, ALU.mult))
            dve.wait_ge(p_lw, 1)
            dve.tensor_copy(wo_s[:], ws[0:D + 1, 0, 0, :]).then_inc(d_wo, 1)

            def embed(g):
                t0, par = g * GT, g % 2
                dve.wait_ge(g_emb[g], 16 * 3 * GT)
                if t0 % TB == 0:
                    for j in range(3):
                        put(dve.memset(emb[0:j + 1, t0, j, :], 0.0))
                    settle()
                put(dve.tensor_tensor(tsum[:, par], emb[:, t0:t0 + GT, 0, :], emb[:, t0:t0 + GT, 1, :], ALU.add))
                settle()
                put(dve.tensor_tensor(tsum[:, par], tsum[:, par], emb[:, t0:t0 + GT, 2, :], ALU.add))

            def residual(g):
                dve.wait_ge(p_wo, g + 1)
                dve.tensor_tensor(h2[:, tiles(g), :], h2[:, tiles(g), :], ws[:, 0], ALU.add).then_inc(d_res, 1)

            def causal(g):
                dve.wait_ge(p_sc, g + 1)
                dve.tensor_tensor(pt[:], sc[:], bc_mid(mask, [P, GT, P]), ALU.mult).then_inc(d_mask, 1)

            def state(g):
                dve.wait_ge(p_st, g + 1)
                for t in range(GT):
                    n = g * GT + t
                    if n + 1 == NT:
                        continue
                    new, old = st[:, (n + 1) % (2 * GT), :], st[:, n % (2 * GT), :]
                    if n % TB == 0:
                        ins = dve.tensor_copy(new, ws[:, 1, t, :])
                    else:
                        dve.wait_ge(d_state, n)
                        ins = dve.tensor_tensor(new, ws[:, 1, t, :], old, ALU.add)
                    ins.then_inc(d_state, 1)

            def split(g):
                bf = pay[:, tiles(g), D:PW].bitcast(BF16)
                p1, p2, p3 = (bf[:, :, n * NW:(n + 1) * NW] for n in range(3))
                w = gw[:, g % 2]
                dve.wait_ge(a_w, g + 1)
                if g == 0:
                    dve.wait_ge(g_clear, 2)
                put(dve.tensor_copy(p1, w))
                settle()
                put(dve.tensor_tensor(gr[:], w, p1, ALU.subtract))
                settle()
                put(dve.tensor_copy(p2, gr[:]))
                settle()
                dve.tensor_tensor(p3, gr[:], p2, ALU.subtract).then_inc(d_pay, 1)

            def layernorms(a, r, f):
                jobs = []
                if 0 <= a < NG:
                    jobs.append((0, tsum[:, a % 2], xln[:, a % 2], d_xln))
                if 0 <= f < NG:
                    dve.wait_ge(d_res, f + 1)
                    jobs.append((2, h2[:, tiles(f), :], pay[:, tiles(f), 0:D], d_xf))
                if 0 <= r < NG:
                    jobs.append((1, vr[:, 1], nrm[:], d_nrm))
                settle()
                for n, src, _, _ in jobs:
                    if n == 1:
                        dve.wait_ge(p_retr, r + 1)
                    for t in range(GT):
                        put(dve.bn_stats(bn[:, n * GT + t, :], src[:, t, :]))
                settle()
                for n, _, _, _ in jobs:
                    for t in range(n * GT, (n + 1) * GT):
                        put(dve.bn_aggr(mv[:, t, :], bn[:, t, :]))
                settle()
                c0, c1 = min(n for n, *_ in jobs) * GT, (max(n for n, *_ in jobs) + 1) * GT
                e0 = C["EPS"] + (r % (TB // GT) if 0 <= r < NG else 0) * 3 * GT
                v, y, a2, b2, i2 = (q[:, c0:c1] for q in (rv, ry, ra, rb, ri))
                put(dve.tensor_tensor(v, mv[:, c0:c1, 1], cw[:, e0 + c0:e0 + c1], ALU.add))
                settle()
                put(dve.tensor_single_scalar(i2, v.bitcast(I32), 1, op=ALU.logical_shift_right))
                settle()
                put(dve.tensor_scalar(y.bitcast(I32), i2, -1.0, float(0x5F3759DF), ALU.mult, ALU.add))
                settle()
                for _ in range(3):
                    put(dve.tensor_tensor(a2, y, y, ALU.mult))
                    settle()
                    put(dve.scalar_tensor_tensor(out=b2, in0=a2, scalar=-0.5, in1=v, op0=ALU.mult, op1=ALU.mult))
                    settle()
                    put(dve.scalar_tensor_tensor(out=y, in0=b2, scalar=1.5, in1=y, op0=ALU.add, op1=ALU.mult))
                    settle()
                for n, src, dst, done in sorted(jobs, key=lambda q: q[0]):
                    if n == 1 and r:
                        dve.wait_ge(p_nT, r)
                    for t in range(GT):
                        c = n * GT + t
                        ins = dve.tensor_scalar(dst[:, t, :], src[:, t, :], mv[:, c, 0:1], ry[:, c:c + 1], ALU.subtract, ALU.mult)
                        if t < GT - 1:
                            put(ins)
                        else:
                            ins.then_inc(done, 1)

            def keep(g):
                dve.wait_ge(d_xln, g + 1)
                put(dve.scalar_tensor_tensor(out=h2[:, tiles(g), :], in0=tsum[:, g % 2], scalar=0.25, in1=xln[:, g % 2],
                                             op0=ALU.mult, op1=ALU.add))

            def descend(level):
                w = 1 << level
                sc_l = tree[:, :, w - 1:2 * w - 1]
                kids = path[:, :, 2 * w - 1:4 * w - 1].rearrange("p t (j s) -> p t j s", s=2)
                if level == 0:
                    put(dve.tensor_scalar(path[:, :, 2:3], sc_l, 0.0, None, ALU.is_gt))
                    put(dve.tensor_scalar(path[:, :, 1:2], sc_l, 0.0, None, ALU.is_le))
                else:
                    here = path[:, :, w - 1:2 * w - 1]
                    put(dve.scalar_tensor_tensor(out=kids[:, :, :, 1], in0=sc_l, scalar=0.0, in1=here,
                                                 op0=ALU.is_gt, op1=ALU.mult))
                    settle()
                    put(dve.tensor_tensor(kids[:, :, :, 0], here, kids[:, :, :, 1], ALU.subtract))
                settle()

            def walk_top(g):
                dve.wait_ge(p_tree, g + 1)
                put(dve.tensor_copy(lg[:, :, 0], tree[:, :, 0]))
                for level in range(0, 4):
                    descend(level)

            def reduce_phase(g):
                dve.wait_ge(a_tk, g + 1)
                dve.wait_ge(a_tq, g + 1)
                put(dve.tensor_scalar(pu[:], ph[:], const("FREQ"), const("OFF"), ALU.mult, ALU.add))
                settle()
                if g:
                    dve.wait_ge(a_sin, g)
                put(dve.tensor_scalar(pr[:], pu[:], ROUND, ROUND, ALU.add, ALU.subtract))
                settle()
                dve.tensor_tensor(pr[:], pu[:], pr[:], ALU.subtract).then_inc(d_phase, 1)

            def walk_rest(g):
                descend(4)
                descend(5)
                dve.tensor_copy(one[:, tiles(g), :], path[:, :, PAR - 1:2 * PAR - 1]).then_inc(d_one, 1)
                descend(6)
                dve.tensor_tensor(pscore[:, :, 1:NODES], tree[:, :, 1:NODES], path[:, :, 1:NODES], ALU.mult).then_inc(d_read, 1)
                dve.wait_ge(d_read, g + 1)
                for level in range(1, 7):
                    w = 1 << level
                    col = 8 if level == 6 else level
                    put(dve.tensor_reduce(lg[:, :, col], pscore[:, :, w - 1:2 * w - 1], AXX, ALU.add))
                put(dve.tensor_reduce(lg[:, :, 6:8], pscore[:, :, 127:255].rearrange("p t (j s) -> p t s j", s=2), AXX, ALU.add))
                settle()
                if g >= 2:
                    dve.wait_ge(a_w, g - 1)
                dve.scalar_tensor_tensor(out=la[:, g % 2], in0=lg[:], scalar=-1.0, in1=lg[:],
                                         op0=ALU.mult, op1=ALU.max).then_inc(d_walk, 1)

            def place(g):
                t0 = g * GT
                dve.wait_ge(p_rank, g + 1)
                dve.wait_ge(d_one, g + 1)
                dve.tensor_tensor(rtmp[:], mm[:, 0, 0:GT * PAR].rearrange("p (t w) -> p t w", t=GT), one[:, tiles(g), :],
                                  ALU.mult).then_inc(d_rank, 1)
                put(dve.tensor_tensor(lpart[:], one[:, t0, :], one[:, t0 + 1, :], ALU.add))
                dve.wait_ge(d_rank, g + 1)
                put(dve.tensor_reduce(row0[:, tiles(g)], rtmp[:], AXX, ALU.add))
                settle()
                put(dve.tensor_scalar(far[:], row0[:, tiles(g)], float(OV0), float(FAR), ALU.is_ge, ALU.mult))
                put(dve.tensor_tensor(lpart[:], lpart[:], one[:, t0 + 2, :], ALU.add))
                settle()
                put(dve.tensor_tensor(lpart[:], lpart[:], one[:, t0 + 3, :], ALU.add))
                settle()
                put(dve.tensor_tensor(lsum[:], lsum[:], lpart[:], ALU.add))
                dve.tensor_tensor(idx1[:, tiles(g)], row0[:, tiles(g)], far[:], ALU.add).then_inc(d_slot, 1)

            for k in range(NG + 4):
                a, r, f, w, s = (k - n for n in range(5))
                if a < NG:
                    embed(a)
                if 0 <= f < NG:
                    residual(f)
                if 0 <= r < NG:
                    causal(r)
                    state(r)
                if 0 <= s < NG:
                    split(s)
                if 0 <= f < NG or 0 <= r < NG or a < NG:
                    layernorms(a, r, f)
                if a < NG:
                    keep(a)
                if 0 <= w < NG:
                    walk_top(w)
                if a < NG:
                    reduce_phase(a)
                if 0 <= w < NG:
                    walk_rest(w)
                    place(w)

            dve.wait_ge(p_cnt, 1)
            put(dve.tensor_copy(onesb[:], ident))
            put(dve.tensor_scalar(ovi[:], vr[:, 0, 0, :], float(P - 1), None, ALU.add))
            put(dve.tensor_scalar(oci[:], vr[0:PAR, 0, 1, 0:1], float(P - 1), None, ALU.add))
            settle()
            put(dve.tensor_single_scalar(ovi[:], ovi[:], 7, op=ALU.logical_shift_right))
            put(dve.tensor_single_scalar(oci[:], oci[:], 7, op=ALU.logical_shift_right))
            settle()
            dve.tensor_scalar(oce[:], oci[:], -1.0, 0.0, ALU.add, ALU.max).then_inc(d_ovc, 1)
            put(dve.tensor_scalar(ovr[:], ovi[:], -1.0, 0.0, ALU.add, ALU.max))
            settle()
            put(dve.tensor_tensor_scan(ovinc[:], onesf[:], ovr[:], 0.0, ALU.mult, ALU.add))
            settle()
            put(dve.tensor_tensor(ovexc[:], ovinc[:], ovr[:], ALU.subtract))
            dve.wait_ge(p_ovi, 1)
            put(dve.tensor_copy(occ[:], vr[0:PAR, 0, 1, 1:2]))
            settle()
            dve.tensor_scalar(cmp[:], iota[0:PAR, 0:OVP], occ[:], None, ALU.is_ge).then_inc(d_cmp, 1)
            put(dve.tensor_scalar(pgi[0:1, OVP:OVP + 1], ovinc[0:1, PAR - 1:PAR], 1.0, None, ALU.max))
            dve.wait_ge(p_pg, 1)
            dve.tensor_scalar(pgi[0:1, 0:OVP], vr[0:1, 0, 2, 0:OVP], float(PAR - 1), None, ALU.min).then_inc(d_pg, 1)
            tmp = ys[:].rearrange("p a d -> p (a d)")[:, 0:NT * PAR].rearrange("p (t w) -> p t w", t=NT)
            put(dve.tensor_tensor(tmp, one[:], bc_mid(ovexc[:], [P, NT, PAR]), ALU.mult))
            put(dve.tensor_copy(tki[:, 0, :], row0[:]))
            put(dve.tensor_scalar(tk[:, 3, :], row0[:], float(OV0), None, ALU.is_ge))
            settle()
            put(dve.tensor_reduce(tk[:, 0, :], tmp, AXX, ALU.add))
            put(dve.tensor_single_scalar(tki[:, 1, :], tki[:, 0, :], 13, op=ALU.logical_shift_right))
            put(dve.tensor_scalar(tki[:, 2, :], tki[:, 0, :], 6, P - 1, ALU.logical_shift_right, ALU.bitwise_and))
            settle()
            put(dve.scalar_tensor_tensor(out=tk[:, 1, :], in0=tki[:, 2, :], scalar=float(OVP), in1=tk[:, 0, :],
                                         op0=ALU.mult, op1=ALU.add))
            put(dve.tensor_scalar(tk[:, 4, :], tk[:, 3, :], -float(FAR), float(FAR), ALU.mult, ALU.add))
            settle()
            put(dve.scalar_tensor_tensor(out=tk[:, 2, :], in0=tki[:, 1, :], scalar=float(OV0 - 1), in1=tk[:, 1, :],
                                         op0=ALU.add, op1=ALU.add))
            settle()
            dve.tensor_tensor(idx2[:], tk[:, 2, :], tk[:, 4, :], ALU.add).then_inc(d_idx2, 1)
            put(dve.tensor_tensor(tk[:, 1, :], tk[:, 2, :], row0[:], ALU.subtract))
            settle()
            put(dve.tensor_tensor(tk[:, 1, :], tk[:, 1, :], tk[:, 3, :], ALU.mult))
            settle()
            put(dve.tensor_tensor(idx3[:], tk[:, 1, :], row0[:], ALU.add))
            settle()

            def products(n, b, xa, xc):
                z, w = zT[:, b], gps[b][:, 0:5 * P].rearrange("p (c s) -> p c s", c=5)
                dve.tensor_tensor(z[:, 0:4, :], w[:, 0:4, :], bc_mid(xa, [P, 4, P]), ALU.mult)
                dve.tensor_tensor(z[:, 4, :], w[:, 4, :], xc, ALU.mult).then_inc(d_z, 1)

            def gather_parts(c):
                dve.wait_ge(s_xs, 16 * (c + 1))
                if c >= 2:
                    dve.wait_ge(p_gt, CH // 4 * (c - 1))
                dve.tensor_copy(parts[:, c % 2].rearrange("p (a w) -> p a w", w=GW),
                                xs[:, c * CH:(c + 1) * CH, D:PW].bitcast(BF16)).then_inc(d_parts, 1)

            put(dve.memset(xb[D:P], 1.0))
            settle()
            gather_parts(0)
            for n in range(PAR):
                if n % CH == 1 and n + CH < PAR:
                    gather_parts(n // CH + 1)
                dve.wait_ge(p_g, n + 1)
                dve.wait_ge(a_x, n // 4 + 1)
                if n >= 2:
                    dve.wait_ge(p_mm, n - 1)
                products(n, n % 2, x1[:, n // 4 % 2, n % 4, :], xb[:, n // 4 % 2, n % 4, :])
            dve.wait_ge(s_xov, 16)
            npg = dve.value_load(pgi[0:1, OVP:OVP + 1], min_val=1, max_val=OVP)
            with dve.Fori(0, npg) as j:
                page = xov[:, bass.ds(j, 1), :]
                dve.tensor_scalar(xo1[:], page[:, :, 0:D].to_broadcast([P, 2, D]), 1.0, None, ALU.mult)
                dve.tensor_scalar(go1[:].unsqueeze(1), page[:, :, D:PW].bitcast(BF16), 1.0, None, ALU.mult).then_inc(d_ov, 1)
                dve.wait_ge(p_g, j + (PAR + 1))
                products(None, 0, x1[:, 0, 0, :], xb[:, 0, 0, :])
                dve.wait_ge(p_mm, j + (PAR + 1))
                dve.tensor_scalar(yov[:, bass.ds(j, 1), :].rearrange("p a d -> p (a d)"), yps[0][:, 0, :], 1.0, None,
                                  ALU.mult).then_inc(d_yov, 1)

            for g in range(NG):
                dve.wait_ge(g_y[g], 16 * GT)
                dve.tensor_tensor(yg[:, tiles(g), :], yg[:, tiles(g), :], h2[:, tiles(g), :], ALU.add).then_inc(d_out, 1)


def lay_out_small(np, w):
    a = np.zeros((P, C_ALL), np.float32)
    r = np.arange(P)
    a[:, C["ID"]:C["ID"] + P] = r[:, None] == r[None]
    a[:, C["MASK"]:C["MASK"] + P] = r[:, None] <= r[None]
    a[:, C["IOTA"]:C["IOTA"] + P] = r[None]
    a[:, C["FREQ"]] = 2.0 ** (r % K // 16) / 2
    a[:, C["OFF"]] = np.where(r < K, 0.25, 0.0)
    eps = np.empty((P, TB // GT, 3, GT), np.float32)
    eps[:, :, 0], eps[:, :, 2] = 16 * EPS, EPS
    eps[:, :, 1] = EPS * K * (1 + r[:, None, None] + P * np.arange(TB).reshape(TB // GT, GT))
    a[:, C["EPS"]:C["EPS"] + 3 * TB] = eps.reshape(P, 3 * TB)
    sel = a[:, C["SEL"]:C["SEL"] + 5 * P].reshape(P, 5, P)
    for row in range(P):
        if row % GW < 3 * NW:
            n = row % GW % NW
            if n < 8:
                sel[row, n // 2, n % 2 * D:(n % 2 + 1) * D] = 1.0
            else:
                sel[row, 4, 0:D] = 1.0
            sel[row, 4, D + n] = 1.0
    a[:, C["SEL"]:C["SEL"] + 5 * P] = sel.reshape(P, 5 * P)
    a[:D, C["W1"]:C["W1"] + D], a[:D, C["W1"] + D:C["W1"] + P] = w["Wk1"], w["Wq1"]
    for n in range(2):
        a[:D, C["W2"] + n * K:C["W2"] + (n + 1) * K] = w["Wk2"]
        a[D:, C["W2"] + n * K:C["W2"] + (n + 1) * K] = w["Wq2"]
        a[n * K:(n + 1) * K, C["B2K"]] = w["bk2"]
        a[n * K:(n + 1) * K, C["B2Q"]] = w["bq2"]
    a[:D, C["B1"]], a[D:, C["B1"]] = w["bk1"], w["bq1"]
    a[:D, C["WV"]:C["WV"] + D], a[D, C["WV"]:C["WV"] + D] = w["Wv"], w["bv"]
    a[:D, C["WO"]:C["WO"] + D], a[D, C["WO"]:C["WO"] + D] = w["Wo"], w["bo"]
    a[:D, C["TREE"]:C["TREE"] + NODES], a[D, C["TREE"]:C["TREE"] + NODES] = w["w1s"].T, w["b1s"]
    a[:D, C["LNW"]], a[D, C["LNW"]] = w["ln_w"], 1.0
    a[:D, C["LNB"]], a[D, C["LNB"]] = w["ln_b"], 1.0
    return a


def lay_out_nodes(np, w2s, b2s):
    a = np.zeros((P, NBLK, D), np.float32)
    for c0, upper, count in ((W01, 0, 2), (W23, 2, 8), (W45, 4, 32)):
        j = np.arange(count)
        a[:D, c0:c0 + count] = w2s[(1 << upper) - 1 + j // 2].transpose(1, 0, 2)
        a[D:, c0:c0 + count] = w2s[(2 << upper) - 1 + j].transpose(1, 0, 2)
    p = np.arange(PAR)
    a[:D, W7:W7 + PAR] = w2s[127 + 2 * p].transpose(1, 0, 2)
    a[D:, W7:W7 + PAR] = w2s[128 + 2 * p].transpose(1, 0, 2)
    a[:D, W6:W6 + PAR] = w2s[63 + p].transpose(1, 0, 2)
    for level in range(6):
        a[D + level, W6:W6 + PAR] = b2s[(1 << level) - 1 + (p >> (6 - level))]
    a[D + 6, W6:W6 + PAR] = b2s[127 + 2 * p]
    a[D + 7, W6:W6 + PAR] = b2s[128 + 2 * p]
    a[D + 8, W6:W6 + PAR] = b2s[63 + p]
    return a.reshape(P, NBLK * D)


def kernel(**inputs):
    import numpy as np
    import concourse.bacc as bacc
    from concourse.bass_utils import run_bass_kernel_spmd as run

    get = lambda name: np.ascontiguousarray(inputs[name])
    w = {n: get(f"L0_attn_{n}") for n in ("Wk1", "bk1", "Wk2", "bk2", "Wq1", "bq1", "Wq2", "bq2", "Wv", "bv", "ln_w", "ln_b", "Wo", "bo")}
    w["w1s"], w["b1s"] = get("L0_ffn_w1s"), get("L0_ffn_b1s")
    arrays = {
        "ids": get("x"), "emb2": get("L0_tok_emb_2"), "emb3": get("L0_tok_emb_3"), "emb4": get("L0_tok_emb_4"),
        "small": lay_out_small(np, w), "nodes": lay_out_nodes(np, get("L0_ffn_w2s"), get("L0_ffn_b2s")),
    }
    nc = bacc.Bacc("TRN2", target_bir_lowering=False, num_devices=1)
    args = [nc.dram_tensor(n, a.shape, mybir.dt.from_np(a.dtype), kind="ExternalInput").ap() for n, a in arrays.items()]
    out = nc.dram_tensor("out", (B, T, D), F32, kind="ExternalOutput").ap()
    build(nc, *args, out)
    return run(nc, [arrays], core_ids=[0]).results[0]["out"]
```
